# Optimizing a Trainium2 kernel written in Bass

```python
import numpy as np
import jax
import jax.numpy as jnp

def _softmax(x, axis=-1):
    return jax.nn.softmax(x, axis=axis)

def _gelu(x):
    return jax.nn.gelu(x, approximate=True)

def _silu(x):
    return jax.nn.silu(x)

def _sigmoid(x):
    return jax.nn.sigmoid(x)

def _layernorm(x, axis=-1, eps=1e-05):
    m = jnp.mean(x, axis=axis, keepdims=True)
    v = jnp.var(x, axis=axis, keepdims=True)
    return (x - m) / jnp.sqrt(v + eps)

def _scatter_add(tgt, idx, src, axis=0):
    return tgt.at[idx].add(src)

def _segment_sum(src, seg, n):
    return jax.ops.segment_sum(src, seg, n)
kernel_name = 'mk_gnn_preln_d1_gnn_r8_eb6b12'

def setup_inputs(seed: int=0):
    np.random.seed(seed)
    _w = jnp.asarray

    def _rec_inputs():
        import jax
        import jax.numpy as jnp
        _gk = jax.random.key(seed)
        x = -0.0003713 + 1 * jax.random.normal(jax.random.fold_in(_gk, 1), (12500, 128), jnp.float32)
        src = jax.random.randint(jax.random.fold_in(_gk, 2), (400000,), 0, 12500, jnp.int32)
        dst = jnp.minimum((12500 * jax.random.uniform(jax.random.fold_in(_gk, 3), (400000,)) ** 2.0).astype(jnp.int32), 99999)
        _o = jnp.argsort(dst, stable=True)
        src = src[_o]
        dst = dst[_o]
        edge_attr_64 = -8.16379e-05 + 0.999858 * jax.random.normal(jax.random.fold_in(_gk, 12), (400000, 64), jnp.float32)
        return (x, src, dst, edge_attr_64)
    x, src, dst, edge_attr_64 = _rec_inputs()

    def _L0_gnn_setup():
        import jax, jax.numpy as jnp
        import numpy as np
        N_NODES = 12500
        N_EDGES = 200000
        NDIM_IN = 128
        EDIMS = 64
        NDIM_OUT = 128
        NUM_HEADS = 4
        HEAD_DIM = NDIM_OUT // NUM_HEADS
        key = jax.random.key(seed)
        ks = jax.random.split(key, 10)
        in_dim = NDIM_IN + EDIMS
        b1 = float(np.sqrt(6.0 / (in_dim + NDIM_OUT)))
        b2 = float(np.sqrt(6.0 / (NDIM_OUT + NDIM_OUT)))
        bav = float(np.sqrt(6.0 / (NUM_HEADS + HEAD_DIM)))
        return {'nfeats': jax.random.normal(ks[0], (N_NODES, NDIM_IN), dtype=jnp.float32), 'efeats': jax.random.normal(ks[1], (N_EDGES, EDIMS), dtype=jnp.float32), 'src': jax.random.randint(ks[2], (N_EDGES,), 0, N_NODES, dtype=jnp.int32), 'dst': jax.random.randint(ks[3], (N_EDGES,), 0, N_NODES, dtype=jnp.int32), 'W_proj_w': jax.random.uniform(ks[4], (NDIM_OUT, in_dim), jnp.float32, -b1, b1), 'W_proj_b': jnp.zeros((NDIM_OUT,), jnp.float32), 'attn_vec': jax.random.uniform(ks[5], (NUM_HEADS, HEAD_DIM), jnp.float32, -bav, bav), 'W_out_w': jax.random.uniform(ks[6], (NDIM_OUT, NDIM_OUT), jnp.float32, -b2, b2), 'W_out_b': jnp.zeros((NDIM_OUT,), jnp.float32), 'ln_gamma': jnp.ones((NDIM_OUT,), jnp.float32), 'ln_beta': jnp.zeros((NDIM_OUT,), jnp.float32)}
    _L0_gnn_all = _L0_gnn_setup()
    _L0_gnn_in = {k: v for k, v in _L0_gnn_all.items() if k in ('W_proj_w', 'W_proj_b', 'attn_vec', 'W_out_w', 'W_out_b', 'ln_gamma', 'ln_beta')}
    del _L0_gnn_all
    return {'x': x, 'src': src, 'dst': dst, 'edge_attr_64': edge_attr_64, 'L0_gnn_W_proj_w': _L0_gnn_in['W_proj_w'], 'L0_gnn_W_proj_b': _L0_gnn_in['W_proj_b'], 'L0_gnn_attn_vec': _L0_gnn_in['attn_vec'], 'L0_gnn_W_out_w': _L0_gnn_in['W_out_w'], 'L0_gnn_W_out_b': _L0_gnn_in['W_out_b'], 'L0_gnn_ln_gamma': _L0_gnn_in['ln_gamma'], 'L0_gnn_ln_beta': _L0_gnn_in['ln_beta']}

def reference(x, src, dst, edge_attr_64, L0_gnn_W_proj_w, L0_gnn_W_proj_b, L0_gnn_attn_vec, L0_gnn_W_out_w, L0_gnn_W_out_b, L0_gnn_ln_gamma, L0_gnn_ln_beta):
    import jax
    import jax.numpy as jnp

    def _L0_gnn_ref(nfeats, efeats, src, dst, W_proj_w, W_proj_b, attn_vec, W_out_w, W_out_b, ln_gamma, ln_beta):
        import jax, jax.numpy as jnp
        import numpy as np
        N_NODES = 12500
        N_EDGES = 200000
        NDIM_IN = 128
        EDIMS = 64
        NDIM_OUT = 128
        NUM_HEADS = 4
        HEAD_DIM = NDIM_OUT // NUM_HEADS
        N = nfeats.shape[0]
        H, D = attn_vec.shape
        x = jnp.concatenate([nfeats[src], efeats], axis=1)
        x_proj = (x @ W_proj_w.T + W_proj_b).reshape(-1, H, D)
        e = jnp.sum(x_proj * attn_vec, axis=-1)
        emax = jax.ops.segment_max(e, dst, num_segments=N)
        ex = jnp.exp(e - emax[dst])
        denom = jax.ops.segment_sum(ex, dst, num_segments=N)
        alpha = ex / denom[dst]
        m = (x_proj * alpha[:, :, None]).reshape(-1, H * D)
        h_neigh = jax.ops.segment_sum(m, dst, num_segments=N)
        h = jax.nn.relu((h_neigh + nfeats) @ W_out_w.T + W_out_b)
        mu = jnp.mean(h, axis=-1, keepdims=True)
        var = jnp.mean((h - mu) ** 2, axis=-1, keepdims=True)
        return (h - mu) * jax.lax.rsqrt(var + 1e-05) * ln_gamma + ln_beta
    h = jnp.maximum(_layernorm(x, axis=-1), 0.0)
    x = x + _L0_gnn_ref(h, edge_attr_64, src, dst, L0_gnn_W_proj_w, L0_gnn_W_proj_b, L0_gnn_attn_vec, L0_gnn_W_out_w, L0_gnn_W_out_b, L0_gnn_ln_gamma, L0_gnn_ln_beta)
    return x

_drawn_inputs = setup_inputs


def setup_inputs(seed=0):
    import zlib

    import numpy as np

    out = dict(_drawn_inputs(seed))
    spreads = {'L0_gnn_W_proj_b': (0.0, 0.1),
     'L0_gnn_W_out_b': (0.0, 0.1),
     'L0_gnn_ln_gamma': (1.0, 0.2),
     'L0_gnn_ln_beta': (0.0, 0.1)}
    factors = {}
    for name, (base, spread) in spreads.items():
        noise = np.random.default_rng([zlib.crc32(name.encode()), seed]).standard_normal(out[name].shape)
        drawn = base * np.exp(spread * noise) if base else spread * noise
        out[name] = jnp.asarray(drawn.astype(out[name].dtype))
    for name, factor in factors.items():
        out[name] = (out[name] * factor).astype(out[name].dtype)
    return out
```

```python
from contextlib import ExitStack

import concourse.bass as bass
from concourse import mybir

P = 128
HEADS = 4
D = 128
ED = 64
HD = D // HEADS
TW = D + HEADS
UW = TW + 1
TILES = 25
GH = HEADS * TILES
SE = TILES * P
CT = 3
CHUNKS = -(-TILES // CT)
LAG = 4
BIG = 1.0e30
EPS = 1e-5
GRP = 4

ALU = mybir.AluOpType
ACT = mybir.ActivationFunctionType
F32 = mybir.dt.float32
I32 = mybir.dt.int32


def chunk_tiles(c):
    return range(c * CT, min(c * CT + CT, TILES))


def node_rows(n):
    return max(p for p in range(1, P + 1) if n % p == 0)


def gnn_layer(nc, x, meta, seg, dq, ef, w_nat, w_t, b_proj, attn, wo_t, b_out, gamma, beta, out):
    N = x.shape[0]
    NS = meta.shape[0]
    NP = node_rows(N)
    NC = N // NP
    assert NS <= P and NS >= 5 and NS % 2 == 1 and NC % GRP == 0
    NG = NC // GRP
    BLK = -(-min(N, NS * SE) // P)
    NT = NS * TILES
    PAIRS = (NS - 2) // 2
    LEFT = (NS - 2) % 2

    with ExitStack() as ctx:
        def sb(name, shape, dt=F32):
            return ctx.enter_context(nc.sbuf_tensor(name, shape, dt))

        def sem(name):
            return ctx.enter_context(nc.semaphore(name))

        table = nc.dram_tensor("table_dram", (N, TW), F32, kind="Internal").ap()
        neigh = nc.dram_tensor("neigh_dram", (N, D), F32, kind="Internal").ap()
        boff_dram = nc.dram_tensor("boff_dram", (NS, TILES), I32, kind="Internal").ap()

        ps = [ctx.enter_context(nc.psum_tensor(f"ps{i}", [P, 512], F32)) for i in range(8)]
        e_ps = ps[0:2]
        agg_ps = ps[2:5]
        lt_ps, pw_ps, sm_ps = ps[5], ps[6], ps[7]

        UC = max((BLK + 1) * UW, NC * TW)
        U = sb("U", [P, UC])
        h = sb("h", [P, NC * D])
        WK = max(2 * TILES * UW + 2 * SE, 4 * SE + 1, NC * D)
        work = sb("work", [P, WK])
        G = [work[:, q * TILES * UW:(q + 1) * TILES * UW].rearrange("p (t w) -> p t w", w=UW) for q in range(2)]
        ef_sb = [work[0:ED, 2 * TILES * UW + q * SE:2 * TILES * UW + (q + 1) * SE] for q in range(2)]
        ncrel_all = sb("ncrel_all", [P, TILES, NS])
        boff = [sb(f"boff{q}", [1, TILES], I32) for q in range(2)]
        meta_sb = [sb(f"meta{q}", [P, 3 * TILES], I32) for q in range(2)]
        seg_sb = [sb(f"seg{q}", [GH, P + 2], I32) for q in range(2)]
        ncrel = [sb(f"ncrel{q}", [P, TILES]) for q in range(2)]
        started = sb("started", [P, TILES])
        ne = sb("ne", [GH, 2, P])
        cut = sb("cut", [GH, 2, P])
        cutmin = sb("cutmin", [GH, 2])
        lc = sb("lc", [P, GH])
        pre = sb("pre", [GH, P])
        suf = sb("suf", [GH, P])
        pre2 = sb("pre2", [GH, P])
        suf2 = sb("suf2", [GH, P])
        mx = sb("mx", [GH, P])
        dd = sb("dd", [GH, P])
        pt = sb("pt", [GH, P])
        ext = sb("ext", [1, 4, HEADS, TILES + 2])
        carry = sb("carry", [1, 2, 4 * (TILES + 2) + 4])
        ccomp = sb("ccomp", [1, 2 * GH])
        cinit = sb("cinit", [GH, 2])
        cont = sb("cont", [1, 1])
        hot = sb("hot", [1, P])
        dr = sb("dr", [1, HEADS])
        dr2 = sb("dr2", [1, HEADS])
        rr = sb("rr", [1, HEADS])
        r1 = sb("r1", [1, HEADS])
        fac = sb("fac", [P, HEADS])
        dist = [sb(f"dist{i}", [P, CT, 2 * P]) for i in range(2)]
        sel = [sb(f"sel{i}", [P, CT, 2 * P]) for i in range(3)]
        ident = sb("ident", [P, P])
        tri = sb("tri", [P, P])
        iota = sb("iota", [P, 2 * P])
        wx = sb("wx", [P, TW])
        we = sb("we", [ED, TW])
        wnat = sb("wnat", [P, D + ED])
        ablk = sb("ablk", [P, HEADS])
        bcol = sb("bcol", [P, 1])
        bwide = sb("bwide", [P, P])
        ones = sb("ones", [P, P])
        bias = sb("bias", [P, TW])
        wo = sb("wo", [P, D])
        bo = sb("bo", [1, D])
        gam = sb("gam", [P, D])
        bet = sb("bet", [P, D])
        stats = sb("stats", [P, GRP, 6])
        mv = sb("mv", [P, NC, 2])
        sd = sb("sd", [P, NC])
        rstd = sb("rstd", [P, NC])
        nmr = sb("nmr", [P, NC])
        colT = [sb(f"colT{i}", [P, GRP * P]) for i in range(2)]
        act_o = [sel[i][:].rearrange("p t n -> p (t n)")[:, 0:GRP * D] for i in range(2)]
        res = [dist[i][:].rearrange("p t n -> p (t n)")[:, 0:GRP * D] for i in range(2)]
        off = sb("off", [P, 1])
        cst = sb("cst", [P, TILES], I32)
        bint = sb("bint", [P, TILES], I32)
        boffs = sb("boffs", [P, TILES], I32)
        base = sb("base", [P, TILES])
        ids_flat = ncrel_all[:].rearrange("p t s -> p (t s)")
        LB = BLK * HEADS
        den = ids_flat[:, 0:LB] if TILES * NS >= 10 * BLK else sb("den", [P, LB])
        rden = ids_flat[:, LB:2 * LB] if TILES * NS >= 10 * BLK else sb("rden", [P, LB])
        empty = ids_flat[:, 2 * LB:2 * LB + BLK] if TILES * NS >= 10 * BLK else sb("empty", [P, BLK])
        rowf = ids_flat[:, 2 * LB + BLK:2 * LB + 2 * BLK] if TILES * NS >= 10 * BLK else sb("rowf", [P, BLK])
        rowi = sb("rowi", [P, BLK], I32)

        s_w = sem("s_w")
        s_blk = sem("s_blk")
        s_pass = {e: sem(f"s_pass{i}") for i, e in enumerate(
            (nc.sync.engine, nc.gpsimd.engine, nc.tensor.engine, nc.vector.engine))}
        s_const = sem("s_const")
        s_x = sem("s_x")
        s_dq = sem("s_dq")
        s_a = sem("s_a")
        s_aw = sem("s_aw")
        s_ac = sem("s_ac")
        s_hT = sem("s_hT")
        s_hTc = sem("s_hTc")
        s_hp = sem("s_hp")
        s_tab = sem("s_tab")
        s_tout = sem("s_tout")
        s_seg = sem("s_seg")
        s_segt = sem("s_segt")
        s_segc = sem("s_segc")
        s_boff = sem("s_boff")
        s_z = sem("s_z")
        s_u0 = sem("s_u0")
        s_meta = [sem(f"s_meta{q}") for q in range(2)]
        s_seg_in = [sem(f"s_seg_in{q}") for q in range(2)]
        s_off = [sem(f"s_off{q}") for q in range(2)]
        s_ef = [sem(f"s_ef{q}") for q in range(2)]
        s_gat = [[sem(f"s_gat{q}_{c}") for c in range(CHUNKS)] for q in range(2)]
        s_e = sem("s_e")
        s_add = sem("s_add")
        s_id = sem("s_id")
        s_cut = sem("s_cut")
        s_lc = sem("s_lc")
        s_lt = sem("s_lt")
        s_ncr = sem("s_ncr")
        s_sc1 = sem("s_sc1")
        s_smt = sem("s_smt")
        s_car = sem("s_car")
        s_cint = sem("s_cint")
        s_mx = sem("s_mx")
        s_exp = sem("s_exp")
        s_pw = sem("s_pw")
        s_pc = sem("s_pc")
        s_r = sem("s_r")
        s_rx = sem("s_rx")
        s_rf = sem("s_rf")
        s_f = sem("s_f")
        s_dist = sem("s_dist")
        s_sel = sem("s_sel")
        s_agg = sem("s_agg")
        s_acc = sem("s_acc")
        s_usc = sem("s_usc")
        s_n = sem("s_n")
        s_nb = sem("s_nb")
        s_sca = sem("s_sca")
        s_zin = sem("s_zin")
        s_y = sem("s_y")
        s_yT = sem("s_yT")
        s_yTc = sem("s_yTc")
        s_o = sem("s_o")
        s_re = sem("s_re")
        s_dv = sem("s_dv")
        s_sq = sem("s_sq")
        s_res = sem("s_res")
        s_out = [sem(f"s_out{i}") for i in range(2)]

        block = ctx.enter_context(nc.Block())

        x_cols = x.rearrange("(p c) d -> p (c d)", c=NC)
        out_cols = out.rearrange("(p c) d -> p (c d)", c=NC)
        XL = 5 if NC % 5 == 0 and (NC // 5) % GRP == 0 else 1
        XC = NC // XL
        WLOADS = 13
        dq_v = work[:, 0:SE + 1].bitcast(I32)
        st_v = work[:, SE + 1:2 * SE + 1]
        c_v = work[:, 2 * SE + 1:3 * SE + 1]
        nc_v = work[:, 3 * SE + 1:4 * SE + 1]
        BPT = 512 // NS if NS >= 8 else 4
        BT = min(BPT, 4)
        NBT = -(-TILES // BT)
        SB_STEPS = 9

        def settle(eng):
            eng.sem_inc(s_pass[eng.engine], 1)

        @block.sync
        def _(sp):
            for c in range(XL):
                sp.dma_start(h[0:NP, c * XC * D:(c + 1) * XC * D],
                             x_cols[:, c * XC * D:(c + 1) * XC * D]).then_inc(s_x, 16)
                sp.wait_ge(s_x, 16 * (c + 1))
                if c == 0:
                    sp.dma_start(wnat[:], w_nat).then_inc(s_w, 16)
                    sp.dma_start(wx[:, 0:D], w_t[0:D, :]).then_inc(s_w, 16)
                    sp.dma_start(we[:, 0:D], w_t[D:D + ED, :]).then_inc(s_w, 16)
                    sp.wait_ge(s_blk, 1)
                    for i in range(HEADS):
                        sp.dma_start(ablk[i * HD:(i + 1) * HD, i:i + 1],
                                     attn[i:i + 1, :].rearrange("a d -> d a")).then_inc(s_w, 16)
                    sp.dma_start(bcol[:], b_proj.rearrange("a d -> d a")).then_inc(s_w, 16)
                    sp.dma_start(bias[:, 0:D], b_proj.to_broadcast([P, D])).then_inc(s_w, 16)
                    sp.dma_start(wo[:], wo_t).then_inc(s_w, 16)
                    sp.dma_start(bo[:], b_out).then_inc(s_w, 16)
                    sp.dma_start(gam[:], gamma.to_broadcast([P, D])).then_inc(s_w, 16)
                    sp.dma_start(bet[:], beta.to_broadcast([P, D])).then_inc(s_w, 16)
                    sp.dma_start(dq_v[0:NS, :], dq).then_inc(s_dq, 16)
            sp.wait_ge(s_seg, 8)
            sp.dma_start(boff_dram, boffs[0:NS, :]).then_inc(s_boff, 16)
            sp.wait_ge(s_tab, NG)
            sp.dma_start(table.rearrange("(p c) w -> p (c w)", c=NC), U[0:NP, 0:NC * TW]).then_inc(s_tout, 16)
            sp.wait_ge(s_u0, 1)
            sp.dma_start(neigh.rearrange("(p c) d -> p (c d)", c=NC), U[0:NP, 0:NC * D]).then_inc(s_z, 16)

            def loads(s, q):
                peel = isinstance(s, int)
                if not peel or s >= 2:
                    sp.wait_ge(s_add, (s - 1) * CHUNKS)
                    settle(sp)
                    sp.wait_ge(s_id, (s - 1) * 2)
                settle(sp)
                sp.dma_start(meta_sb[q][:], meta[bass.ds(s, 1)].rearrange("o p m -> (o p) m")).then_inc(s_meta[q], 16)
                if not peel or s >= 2:
                    sp.wait_ge(s_e, (s - 1) * CHUNKS)
                settle(sp)
                sp.dma_start(ef_sb[q], ef[bass.ds(s, 1)].rearrange("o d e -> (o d) e")).then_inc(s_ef[q], 16)
                if not peel or s >= 2:
                    sp.wait_ge(s_acc, (s - 1) * TILES)
                if peel and s == 0:
                    sp.wait_ge(s_boff, 16)
                settle(sp)
                sp.dma_start(boff[q][:], boff_dram[bass.ds(s, 1), :]).then_inc(s_off[q], 16)
                if not peel or s >= 2:
                    sp.wait_ge(s_r, (s - 1) * 5)
                    settle(sp)
                    sp.wait_ge(s_cut, (s - 1) * 4)
                settle(sp)
                sp.dma_start(seg_sb[q][:], seg[bass.ds(s, 1)].rearrange("o r e -> (o r) e")).then_inc(s_seg_in[q], 16)

            sp.wait_ge(s_segt, 1 + NBT)
            loads(0, 0)
            loads(1, 1)
            with sp.Fori(0, PAIRS) as k:
                loads(k * 2 + 2, 0)
                loads(k * 2 + 3, 1)
            if LEFT:
                loads(NS - 1, (NS - 1) % 2)
            sp.wait_ge(s_agg, NT)
            sp.wait_ge(s_add, NS * CHUNKS)
            sp.dma_start(work[0:NP, 0:NC * D], x_cols).then_inc(s_x, 16)
            sp.wait_ge(s_sca, 16 * BLK)
            for c in range(XL):
                sp.dma_start(U[0:NP, c * XC * D:(c + 1) * XC * D],
                             neigh.rearrange("(p c) d -> p (c d)", c=NC)[:, c * XC * D:(c + 1) * XC * D]
                             ).then_inc(s_zin, 16)
                sp.wait_ge(s_zin, 16 * (c + 1))
            for g in range(NG):
                sp.wait_ge(s_res, 3 * (g + 1))
                sp.dma_start(out_cols[:, g * GRP * D:(g + 1) * GRP * D],
                             res[g % 2][0:NP, :]).then_inc(s_out[g % 2], 16)
            for i in range(2):
                sp.wait_ge(s_out[i], 16 * ((NG + 1 - i) // 2))

        @block.gpsimd
        def _(pool):
            pool.memset(ones[:], 1.0).then_inc(s_const, 1)
            pool.wait_ge(s_const, 1)
            pool.affine_select(out=ident[:], in_=ones[:], compare_op=ALU.is_equal, fill=0.0, base=0,
                               pattern=[[-1, P]], channel_multiplier=1).then_inc(s_const, 1)
            pool.affine_select(out=tri[:], in_=ones[:], compare_op=ALU.is_gt, fill=0.0, base=0,
                               pattern=[[1, P]], channel_multiplier=-1).then_inc(s_const, 1)
            pool.iota(iota[:], pattern=[[1, 2 * P]], base=0, channel_multiplier=0,
                      allow_small_or_imprecise_dtypes=True).then_inc(s_const, 1)
            pool.wait_ge(s_tout, 16)

            def gathers(s, q, turn):
                pool.wait_ge(s_meta[q], (turn + 1) * 16)
                for c in range(CHUNKS):
                    if not isinstance(s, int) or s >= 2:
                        pool.wait_ge(s_agg, (s - 2) * TILES + chunk_tiles(c)[-1] + 1)
                    settle(pool)
                    for t in chunk_tiles(c):
                        pool.indirect_dma_start(G[q][:, t, 0:TW], None, table,
                                                bass.IndirectOffsetOnAxis(ap=meta_sb[q][:, t:t + 1], axis=0)
                                                ).then_inc(s_gat[q][c], 16)

            gathers(0, 0, 0)
            gathers(1, 1, 0)
            with pool.Fori(0, PAIRS) as k:
                gathers(k * 2 + 2, 0, k + 1)
                gathers(k * 2 + 3, 1, k + 1)
            if LEFT:
                gathers(NS - 1, (NS - 1) % 2, (NS - 1) // 2)
            pool.wait_ge(s_z, 16)
            for b in range(BLK):
                pool.wait_ge(s_nb, b + 1)
                pool.indirect_dma_start(neigh, bass.IndirectOffsetOnAxis(ap=rowi[:, b:b + 1], axis=0),
                                        U[:, b * UW:b * UW + D], None,
                                        bounds_check=N - 1, oob_is_err=False).then_inc(s_sca, 16)
            for c in range(XL):
                pool.wait_ge(s_zin, 16 * (c + 1))
                for g in range(c * XC // GRP, (c + 1) * XC // GRP):
                    a, e = g * GRP * D, (g + 1) * GRP * D
                    pool.tensor_tensor(h[0:NP, a:e], h[0:NP, a:e], U[0:NP, a:e], ALU.add).then_inc(s_y, 1)

        @block.tensor
        def _(pe):
            pe.wait_ge(s_const, 4)
            pe.wait_ge(s_w, 16 * WLOADS)
            pe.matmul(ps[7][:, 0:HEADS], wnat[:, 0:D], ablk[:], start=True, stop=True)
            pe.matmul(ps[7][0:ED, 4:4 + HEADS], wnat[:, D:D + ED], ablk[:], start=True, stop=True)
            pe.wait_ge(s_a, 2)
            pe.matmul(ps[7][:, 8:8 + HEADS], bwide[:], ablk[:], start=True, stop=True).then_inc(s_aw, 1)

            def turn_group(g, src, ready, value, done, free, freed):
                pe.wait_ge(ready, value)
                if g >= 2:
                    pe.wait_ge(free, freed)
                for i in range(GRP):
                    j = (g * GRP + i) * D
                    mm = pe.transpose(ps[g % 2][:, i * NP:(i + 1) * NP], src[0:NP, j:j + D], ident[0:NP, 0:NP])
                mm.then_inc(done, 1)

            def rows_group(g):
                pe.wait_ge(s_hTc, g + 1)
                if g == 0:
                    pe.wait_ge(s_a, 5)
                if g >= 2:
                    pe.wait_ge(s_tab, g - 1)
                for i in range(GRP):
                    bank = ps[2 + 2 * (g % 2) + i // 2]
                    mm = pe.matmul(bank[0:NP, (i % 2) * TW:(i % 2) * TW + TW],
                                   colT[g % 2][:, i * NP:(i + 1) * NP], wx[:], start=True, stop=True)
                mm.then_inc(s_hp, 1)

            for g in range(NG + 1):
                if g < NG:
                    turn_group(g, h, s_ac, g + 1, s_hT, s_hTc, g - 1)
                if g >= 1:
                    rows_group(g - 1)
            pe.wait_ge(s_seg, 2)
            pe.matmul(ps[6][0:NS, 0:1], tri[0:NS, 0:NS], c_v[0:NS, SE - 1:SE], start=True, stop=True).then_inc(s_segt, 1)
            pe.wait_ge(s_seg, SB_STEPS)
            for b in range(NBT):
                if b >= 2:
                    pe.wait_ge(s_segc, b - 1)
                if b < 2:
                    pe.wait_ge(s_hTc, NG)
                for i, t in enumerate(range(b * BT, min(b * BT + BT, TILES))):
                    mm = pe.transpose(ps[b % 2][:, i * NS:(i + 1) * NS], nc_v[0:NS, t * P:(t + 1) * P],
                                      ident[0:NS, 0:NS])
                mm.then_inc(s_segt, 1)
            pe.wait_ge(s_segc, NBT)
            pe.wait_ge(s_tab, NG)

            def edge_part(s, q, turn, c):
                peel = isinstance(s, int)
                if c == 0:
                    pe.wait_ge(s_ef[q], (turn + 1) * 16)
                if not peel or s * CHUNKS + c >= 2:
                    pe.wait_ge(s_add, s * CHUNKS + c - 1)
                bank = e_ps[(q * CHUNKS + c) % 2]
                for i, t in enumerate(chunk_tiles(c)):
                    mm = pe.matmul(bank[:, i * TW:(i + 1) * TW], ef_sb[q][:, t * P:(t + 1) * P], we[:],
                                   start=True, stop=True)
                mm.then_inc(s_e, 1)

            def attention(u, step):
                if step == 0:
                    pe.wait_ge(s_lc, u + 1)
                    if not isinstance(u, int) or u >= 1:
                        pe.wait_ge(s_mx, 5 * u)
                    pe.transpose(lt_ps[0:GH, 0:P], lc[:], ident[:]).then_inc(s_lt, 1)
                if step == 1:
                    pe.wait_ge(s_sc1, 2 * u + 2)
                    pe.wait_ge(s_cut, 4 * u + 4)
                    for i, col in enumerate((pre[:, P - 1:P], cutmin[:, 0:1], suf[:, 0:1], cutmin[:, 1:2])):
                        mm = pe.transpose(sm_ps[0:1, i * GH:(i + 1) * GH], col, ident[0:GH, 0:GH])
                    mm.then_inc(s_smt, 1)
                if step == 2:
                    pe.wait_ge(s_car, 4 * u + 4)
                    settle(pe)
                    for i in range(2):
                        mm = pe.transpose(sm_ps[0:GH, 400 + i:401 + i], ccomp[0:1, i * GH:(i + 1) * GH],
                                          ident[0:1, 0:1])
                    mm.then_inc(s_cint, 1)
                if step == 3:
                    pe.wait_ge(s_mx, 5 * u + 4)
                    pe.transpose(sm_ps[0:1, 0:GH], mx[:, 0:1], ident[0:GH, 0:GH])
                    pe.wait_ge(s_exp, u + 1)
                    if not isinstance(u, int) or u >= 1:
                        pe.wait_ge(s_f, CHUNKS * u)
                        pe.wait_ge(s_pc, u)
                    pe.transpose(pw_ps[:, 0:GH], pt[:], ident[0:GH, 0:GH]).then_inc(s_pw, 1)
                if step == 4:
                    pe.wait_ge(s_r, 5 * u + 5)
                    pe.matmul(sm_ps[:, 404:404 + HEADS], hot[0:1, :], r1[0:1, :], start=True, stop=True).then_inc(s_rf, 1)

            def sums(v, cc):
                pe.wait_ge(s_sel, v * CHUNKS + cc + 1)
                pe.wait_ge(s_f, v * CHUNKS + cc + 1)
                if cc == 0:
                    pe.wait_ge(s_pc, v + 1)
                    pe.wait_ge(s_id, v * 2 + 2)
                for t in chunk_tiles(cc):
                    back = 3 if t else 1
                    if not isinstance(v, int) or v * TILES + t >= 3:
                        pe.wait_ge(s_acc, v * TILES + t - back + 1)
                    for b in range(2):
                        mm = pe.matmul(agg_ps[t % 3][:, b * UW:(b + 1) * UW],
                                       sel[cc % 3][:, t - cc * CT, b * P:(b + 1) * P],
                                       G[pe_slot[0]][:, t, :], start=True, stop=True)
                    mm.then_inc(s_agg, 1)

            pe_slot = [0]

            def period(s, q, turn, new=True, att=True, old=True, cur=True, more=True):
                for c in range(CHUNKS):
                    if new and c + 1 < CHUNKS:
                        edge_part(s, q, turn, c + 1)
                    if more and c + 1 == CHUNKS:
                        edge_part(s + 1, 1 - q, turn + q, 0)
                    if att and c < 5:
                        attention(s - 1, c)
                    if c < LAG and old:
                        pe_slot[0] = q
                        sums(s - 2, c + CHUNKS - LAG)
                    if c >= LAG and cur:
                        pe_slot[0] = 1 - q
                        sums(s - 1, c - LAG)

            edge_part(0, 0, 0, 0)
            period(0, 0, 0, att=False, old=False, cur=False)
            period(1, 1, 0, old=False)
            with pe.Fori(0, PAIRS) as k:
                period(k * 2 + 2, 0, k + 1)
                period(k * 2 + 3, 1, k + 1)
            if LEFT:
                period(NS - 1, (NS - 1) % 2, (NS - 1) // 2, more=False)
            period(NS, NS % 2, 0, new=False, more=False)
            period(NS + 1, (NS + 1) % 2, 0, new=False, att=False, cur=False, more=False)
            for g in range(NG + 1):
                if g < NG:
                    turn_group(g, h, s_y, g + 1, s_yT, s_yTc, g - 1)
                if g >= 1:
                    j = g - 1
                    pe.wait_ge(s_yTc, j + 1)
                    if j >= 2:
                        pe.wait_ge(s_re, j - 1)
                    for i in range(GRP):
                        o = ps[2 + j % 2][0:NP, i * D:(i + 1) * D]
                        pe.matmul(o, ones[0:1, 0:NP], bo[0:1, :], start=True, stop=False)
                        mm = pe.matmul(o, colT[j % 2][:, i * NP:(i + 1) * NP], wo[:], start=False, stop=True)
                    mm.then_inc(s_o, 1)

        @block.vector
        def _(dve):
            dve.memset(ablk[:], 0.0).then_inc(s_blk, 1)
            dve.wait_ge(s_w, 16 * WLOADS)
            dve.wait_ge(s_const, 4)
            dve.memset(rowi[:], 0).then_inc(s_a, 1)
            dve.tensor_scalar(bwide[:], ones[:], bcol[:, 0:1], None, ALU.mult).then_inc(s_a, 1)
            dve.wait_ge(s_aw, 1)
            dve.tensor_copy(wx[:, D:TW], ps[7][:, 0:HEADS]).then_inc(s_a, 1)
            dve.tensor_copy(we[:, D:TW], ps[7][0:ED, 4:4 + HEADS]).then_inc(s_a, 1)
            dve.tensor_copy(bias[:, D:TW], ps[7][:, 8:8 + HEADS]).then_inc(s_a, 1)
            dve.wait_ge(s_a, 5)

            def moments(g, src, cols, chain, n0):
                n = n0
                for i in range(GRP):
                    dve.bn_stats(stats[0:NP, i, :], src(i)).then_inc(chain, 1)
                n += GRP
                dve.wait_ge(chain, n)
                for i in range(GRP):
                    dve.bn_aggr(mv[0:NP, cols + i, :], stats[0:NP, i, :]).then_inc(chain, 1)
                n += GRP
                dve.wait_ge(chain, n)
                dve.tensor_scalar(sd[0:NP, cols:cols + GRP], mv[0:NP, cols:cols + GRP, 1], EPS, None,
                                  ALU.add).then_inc(chain, 1)
                return n + 1

            def inverse(cols, sq, value, chain, n):
                dve.wait_ge(sq, value)
                dve.reciprocal(rstd[0:NP, cols:cols + GRP], sd[0:NP, cols:cols + GRP]).then_inc(chain, 1)
                dve.wait_ge(chain, n + 1)
                dve.scalar_tensor_tensor(out=nmr[0:NP, cols:cols + GRP], in0=mv[0:NP, cols:cols + GRP, 0],
                                         scalar=-1.0, in1=rstd[0:NP, cols:cols + GRP],
                                         op0=ALU.mult, op1=ALU.mult).then_inc(chain, 1)
                return n + 2

            def store_rows(g):
                dve.wait_ge(s_hp, g + 1)
                for half in range(2):
                    bank = ps[2 + 2 * (g % 2) + half]
                    c0 = (g * GRP + 2 * half) * TW
                    ins = dve.tensor_tensor(
                        U[0:NP, c0:c0 + 2 * TW].rearrange("p (t w) -> p t w", w=TW),
                        bank[0:NP, 0:2 * TW].rearrange("p (t w) -> p t w", w=TW),
                        bias[0:NP, :].unsqueeze(1).to_broadcast([NP, 2, TW]), ALU.add)
                ins.then_inc(s_tab, 1)

            n = 5
            for g in range(NG):
                c0 = g * GRP
                dve.wait_ge(s_x, 16 * (c0 // XC + 1))
                n = moments(g, lambda i: h[0:NP, (c0 + i) * D:(c0 + i + 1) * D], c0, s_a, n)
                n = inverse(c0, s_sq, g + 1, s_a, n)
                if g >= 1:
                    store_rows(g - 1)
            store_rows(NG - 1)
            STEPS_A = n

            dve.wait_ge(s_dq, 16)
            dve.tensor_tensor(st_v[0:NS, :], dq_v[0:NS, 1:SE + 1], dq_v[0:NS, 0:SE], ALU.not_equal).then_inc(s_seg, 1)
            dve.wait_ge(s_seg, 1)
            dve.tensor_tensor_scan(c_v[0:NS, :], st_v[0:NS, :], st_v[0:NS, :], 0.0, ALU.add, ALU.max).then_inc(s_seg, 1)
            dve.wait_ge(s_segt, 1)
            dve.tensor_copy(off[0:NS, :], ps[6][0:NS, 0:1]).then_inc(s_seg, 1)
            dve.wait_ge(s_seg, 3)
            dve.tensor_scalar(c_v[0:NS, :], c_v[0:NS, :], off[0:NS, 0:1], -1.0, ALU.add, ALU.add).then_inc(s_seg, 1)
            dve.wait_ge(s_seg, 4)
            dve.tensor_copy(cst[0:NS, :], c_v[0:NS, 0:SE:P]).then_inc(s_seg, 1)
            dve.wait_ge(s_seg, 5)
            dve.tensor_scalar(bint[0:NS, :], cst[0:NS, :], 7, None, ALU.logical_shift_right).then_inc(s_seg, 1)
            dve.wait_ge(s_seg, 6)
            dve.tensor_scalar(base[0:NS, :], bint[0:NS, :], float(P), None, ALU.mult).then_inc(s_seg, 1)
            dve.tensor_scalar(boffs[0:NS, :], bint[0:NS, :], float(UW), None, ALU.mult).then_inc(s_seg, 1)
            dve.wait_ge(s_seg, 8)
            dve.tensor_tensor(nc_v[0:NS, :].rearrange("p (t e) -> p t e", e=P),
                              base[0:NS, :].unsqueeze(2).to_broadcast([NS, TILES, P]),
                              c_v[0:NS, :].rearrange("p (t e) -> p t e", e=P), ALU.subtract).then_inc(s_seg, 1)
            dve.wait_ge(s_tout, 16)
            dve.memset(U[:], 0.0).then_inc(s_u0, 1)
            dve.memset(ext[:], -BIG).then_inc(s_u0, 1)
            dve.wait_ge(s_segt, 1 + NBT)
            dve.wait_ge(s_u0, 2)

            def add_chunk(s, q, turn, c):
                ts = chunk_tiles(c)
                dve.wait_ge(s_gat[q][c], (turn + 1) * 16 * len(ts))
                dve.wait_ge(s_e, s * CHUNKS + c + 1)
                rows = G[q][:, ts[0]:ts[-1] + 1, 0:TW]
                dve.tensor_tensor(rows, rows,
                                  e_ps[(q * CHUNKS + c) % 2][:, 0:len(ts) * TW].rearrange("p (t w) -> p t w", w=TW),
                                  ALU.add).then_inc(s_add, 1)

            def node_ids(s, q):
                peel = isinstance(s, int)
                if not peel or s >= 1:
                    dve.wait_ge(s_id, 2 * s)
                cur, before = meta_sb[q][:, TILES:2 * TILES], meta_sb[q][:, 2 * TILES:3 * TILES]
                dve.tensor_tensor(started[:], cur, before, ALU.not_equal).then_inc(s_id, 1)
                if not peel or s >= 2:
                    dve.wait_ge(s_agg, (s - 1) * TILES)
                dve.wait_ge(s_id, 2 * s + 1)
                dve.tensor_tensor(G[q][:, :, UW - 1], started[:], cur, ALU.mult).then_inc(s_id, 1)

            def cuts(s, q, turn):
                dve.wait_ge(s_seg_in[q], (turn + 1) * 16)
                if not isinstance(s, int) or s >= 1:
                    dve.wait_ge(s_cut, 4 * s)
                    dve.wait_ge(s_mx, 5 * s)
                dve.tensor_tensor(ne[:, 0, :], seg_sb[q][:, 1:P + 1], seg_sb[q][:, 0:P], ALU.not_equal).then_inc(s_cut, 1)
                dve.tensor_tensor(ne[:, 1, :], seg_sb[q][:, 1:P + 1], seg_sb[q][:, 2:P + 2],
                                  ALU.not_equal).then_inc(s_cut, 1)
                dve.wait_ge(s_cut, 4 * s + 2)
                dve.tensor_scalar(cut[:], ne[:], -BIG, None, ALU.mult).then_inc(s_cut, 1)
                dve.wait_ge(s_cut, 4 * s + 3)
                dve.tensor_reduce(cutmin[:], cut[:], mybir.AxisListType.X, ALU.min).then_inc(s_cut, 1)

            def scans(pre_o, suf_o, ini_p, ini_s, chain):
                dve.tensor_tensor_scan(pre_o[:], cut[:, 0, :], lt_ps[0:GH, 0:P], ini_p, ALU.add, ALU.max).then_inc(chain, 1)
                dve.tensor_tensor_scan(suf_o[:, ::-1], cut[:, 1, ::-1], lt_ps[0:GH, 0:P][:, ::-1], ini_s,
                                       ALU.add, ALU.max).then_inc(chain, 1)

            EX = HEADS * (TILES + 2)

            def attention(u, q, step):
                if step == 0:
                    dve.wait_ge(s_lt, u + 1)
                    dve.wait_ge(s_cut, 4 * u + 4)
                    scans(pre, suf, -BIG, -BIG, s_sc1)
                if step == 1:
                    dve.wait_ge(s_smt, u + 1)
                    flat = [ext[0:1, i].rearrange("o h t -> o (h t)") for i in range(4)]
                    dve.tensor_copy(ext[0:1, :, :, 1:TILES + 1],
                                    sm_ps[0:1, 0:4 * GH].rearrange("o (k h t) -> o k h t", k=4, h=HEADS)
                                    ).then_inc(s_car, 1)
                    dve.wait_ge(s_car, 4 * u + 1)
                    if not isinstance(u, int) or u >= 1:
                        dve.wait_ge(s_r, 5 * u)
                    dve.tensor_tensor_scan(carry[0:1, 0, 0:EX], flat[1], flat[0], -BIG, ALU.add, ALU.max).then_inc(s_car, 1)
                    dve.tensor_tensor_scan(carry_back[:, ::-1], flat[3][:, ::-1], flat[2][:, ::-1], -BIG,
                                           ALU.add, ALU.max).then_inc(s_car, 1)
                    dve.wait_ge(s_car, 4 * u + 3)
                    dve.tensor_copy(ccomp[0:1, :].rearrange("o (k h t) -> o k h t", k=2, h=HEADS),
                                    carry_view).then_inc(s_car, 1)
                if step == 2:
                    dve.wait_ge(s_cint, u + 1)
                    dve.tensor_copy(cinit[:], sm_ps[0:GH, 400:402]).then_inc(s_mx, 1)
                    dve.wait_ge(s_mx, 5 * u + 1)
                    scans(pre2, suf2, cinit[:, 0:1], cinit[:, 1:2], s_mx)
                    dve.wait_ge(s_mx, 5 * u + 3)
                    dve.tensor_tensor(mx[:], pre2[:], suf2[:], ALU.max).then_inc(s_mx, 1)
                    dve.wait_ge(s_mx, 5 * u + 4)
                    if not isinstance(u, int) or u >= 1:
                        dve.wait_ge(s_exp, u)
                    dve.tensor_tensor(dd[:], lt_ps[0:GH, 0:P], mx[:], ALU.subtract).then_inc(s_mx, 1)
                if step == 3:
                    dve.wait_ge(s_pw, u + 1)
                    dve.tensor_tensor(dr[:], carry[0:1, 0, 0:EX:TILES + 2], sm_ps[0:1, 0:GH:TILES],
                                      ALU.subtract).then_inc(s_r, 1)
                    dve.tensor_tensor(cont[:], seg_sb[q][0:1, 1:2], seg_sb[q][0:1, 0:1], ALU.is_equal).then_inc(s_r, 1)
                    dve.wait_ge(s_r, 5 * u + 2)
                    dve.tensor_scalar(dr2[:], dr[:], cont[0:1, 0:1], None, ALU.mult).then_inc(s_r, 1)
                    dve.tensor_copy(ext[0:1, 0, :, 0], carry[0:1, 0, TILES:EX:TILES + 2]).then_inc(s_r, 1)
                    dve.wait_ge(s_ncr, u + 1)
                    if not isinstance(u, int) or u >= 1:
                        dve.wait_ge(s_rf, u)
                    dve.tensor_scalar(hot[:], iota[0:1, 0:P], ncrel[q][0:1, 0:1], 0.0, ALU.add, ALU.is_equal)
                    dve.wait_ge(s_rx, u + 1)
                    dve.tensor_scalar(r1[:], rr[:], -1.0, None, ALU.add).then_inc(s_r, 1)

            carry_back = carry[:].rearrange("o k x -> o (k x)")[:, EX + 2:2 * EX + 2]
            carry_view = carry[:, :, 0:EX].rearrange("o k (h p) -> o k h p", h=HEADS)[:, :, :, 0:TILES]

            def rescale(u, off0):
                dve.wait_ge(s_rf, u + 1)
                dve.tensor_scalar(fac[:], sm_ps[:, 404:404 + HEADS], 1.0, None, ALU.add).then_inc(s_usc, 1)
                dve.wait_ge(s_usc, 3 * u + 1)
                if not isinstance(u, int) or u >= 1:
                    dve.wait_ge(s_acc, TILES * u)
                num = U[:, bass.ds(off0, D)].rearrange("p (h d) -> p h d", h=HEADS)
                dve.tensor_tensor(num, num, fac[:].unsqueeze(2).to_broadcast([P, HEADS, HD]), ALU.mult).then_inc(s_usc, 1)
                dn = U[:, bass.ds(off0 + D, HEADS)]
                dve.tensor_tensor(dn, dn, fac[:], ALU.mult).then_inc(s_usc, 1)

            def weight(u, q, c0, c1):
                if c0 == 0:
                    dve.wait_ge(s_pw, u + 1)
                    dve.wait_ge(s_add, (u + 1) * CHUNKS)
                    dve.wait_ge(s_lc, u + 1)
                    dve.tensor_copy(G[q][:, :, D:TW],
                                    pw_ps[:, 0:GH].rearrange("p (h t) -> p t h", h=HEADS)).then_inc(s_pc, 1)
                for c in range(c0, c1):
                    ts = chunk_tiles(c)
                    rows = G[q][:, ts[0]:ts[-1] + 1, 0:D].rearrange("p t (h d) -> p t h d", h=HEADS)
                    w = pw_ps[:, 0:GH].rearrange("p (h t) -> p t h", h=HEADS)[:, ts[0]:ts[-1] + 1, :]
                    dve.tensor_tensor(rows, rows, w.unsqueeze(3).to_broadcast([P, len(ts), HEADS, HD]),
                                      ALU.mult).then_inc(s_f, 1)

            def offsets(q, turn, t0, t1):
                dve.wait_ge(s_off[q], (turn + 1) * 16)
                settle(dve)
                return nc.values_load_multi_w_load_instructions(
                    boff[q][0:1, t0:t1], engines=[dve.engine], min_val=0,
                    max_val=(BLK - 1) * UW,
                    skip_runtime_bounds_check_because="compact ids are below the number of nodes")[1]

            def accumulate(v, cc, offs, t0):
                for t in chunk_tiles(cc):
                    dve.wait_ge(s_agg, v * TILES + t + 1)
                    if t == 0:
                        dve.wait_ge(s_usc, 3 * v + 3)
                    if not isinstance(v, int) or v * TILES + t >= 1:
                        dve.wait_ge(s_acc, v * TILES + t)
                    two = U[:, bass.ds(offs[t - t0], 2 * UW)]
                    dve.tensor_tensor(two, two, agg_ps[t % 3][:, 0:2 * UW], ALU.add).then_inc(s_acc, 1)

            F_AT = {4: (0, 2), 5: (2, 4), 6: (4, 6), 7: (6, 8), 8: (8, 9)}

            def period(s, q, turn, new=True, att=True, old=True, cur=True):
                first_old = chunk_tiles(CHUNKS - LAG)[0]
                if old:
                    offs = offsets(q, turn - 1, first_old, TILES)
                for c in range(CHUNKS):
                    if new:
                        add_chunk(s, q, turn, c)
                    if c < LAG and old:
                        accumulate(s - 2, c + CHUNKS - LAG, offs, first_old)
                    if att and c < 4:
                        attention(s - 1, 1 - q, c)
                    if att and c in F_AT:
                        weight(s - 1, 1 - q, *F_AT[c])
                    if c == LAG and cur:
                        offs = offsets(1 - q, turn - 1 + q, 0, first_old)
                        rescale(s - 1, offs[0])
                    if c >= LAG and cur:
                        accumulate(s - 1, c - LAG, offs, 0)
                    if new and c == 5:
                        node_ids(s, q)
                    if new and c == 6:
                        cuts(s, q, turn)

            period(0, 0, 0, att=False, old=False, cur=False)
            period(1, 1, 0, old=False)
            with dve.Fori(0, PAIRS) as k:
                period(k * 2 + 2, 0, k + 1)
                period(k * 2 + 3, 1, k + 1)
            if LEFT:
                period(NS - 1, (NS - 1) % 2, (NS - 1) // 2)
            period(NS, NS % 2, NS // 2, new=False)
            period(NS + 1, (NS + 1) % 2, (NS + 1) // 2, new=False, att=False, cur=False)

            dve.wait_ge(s_acc, NT)
            ub = U[:, 0:BLK * UW].rearrange("p (b w) -> p b w", w=UW)
            den3 = den[:].rearrange("p (b h) -> p b h", h=HEADS)
            rden3 = rden[:].rearrange("p (b h) -> p b h", h=HEADS)
            dve.tensor_scalar(den3, ub[:, :, D:TW], 1.0 / BIG, None, ALU.max).then_inc(s_n, 1)
            dve.tensor_scalar(empty[:], ub[:, :, D], 0.0, float(4 * N), ALU.is_equal, ALU.mult).then_inc(s_n, 1)
            dve.wait_ge(s_n, 2)
            dve.reciprocal(rden[:], den[:]).then_inc(s_n, 1)
            dve.tensor_tensor(rowf[:], empty[:], ub[:, :, UW - 1], ALU.add).then_inc(s_n, 1)
            dve.wait_ge(s_n, 4)
            dve.tensor_copy(rowi[:], rowf[:]).then_inc(s_n, 1)
            dve.wait_ge(s_n, 5)
            for b in range(BLK):
                num = ub[:, b, 0:D].rearrange("p (h d) -> p h d", h=HEADS)
                dve.tensor_tensor(num, num, rden3[:, b, :].unsqueeze(2).to_broadcast([P, HEADS, HD]),
                                  ALU.mult).then_inc(s_nb, 1)
            dve.wait_ge(s_x, 16 * (XL + 1))
            n = 0
            for g in range(NG):
                c0 = g * GRP
                dve.wait_ge(s_re, g + 1)
                n = moments(g, lambda i: act_o[g % 2][0:NP, i * D:(i + 1) * D], c0, s_dv, n)
                n = inverse(c0, s_sq, NG + g + 1, s_dv, n)
                dve.wait_ge(s_dv, n)
                if g >= 2:
                    dve.wait_ge(s_out[g % 2], 16 * (g // 2))
                for i in range(GRP):
                    dve.tensor_scalar(act_o[g % 2][0:NP, i * D:(i + 1) * D], act_o[g % 2][0:NP, i * D:(i + 1) * D],
                                      rstd[0:NP, c0 + i:c0 + i + 1], nmr[0:NP, c0 + i:c0 + i + 1],
                                      ALU.mult, ALU.add).then_inc(s_dv, 1)
                n += GRP
                dve.wait_ge(s_dv, n)
                r3 = res[g % 2][0:NP, :].rearrange("p (t d) -> p t d", d=D)
                a3 = act_o[g % 2][0:NP, :].rearrange("p (t d) -> p t d", d=D)
                dve.tensor_tensor(r3, a3, gam[0:NP, :].unsqueeze(1).to_broadcast([NP, GRP, D]), ALU.mult).then_inc(s_res, 1)
                dve.wait_ge(s_res, 3 * g + 1)
                dve.tensor_tensor(r3, r3, bet[0:NP, :].unsqueeze(1).to_broadcast([NP, GRP, D]), ALU.add).then_inc(s_res, 1)
                dve.wait_ge(s_res, 3 * g + 2)
                dve.tensor_tensor(res[g % 2][0:NP, :], res[g % 2][0:NP, :],
                                  work[0:NP, c0 * D:(c0 + GRP) * D], ALU.add).then_inc(s_res, 1)

        @block.scalar
        def _(act):
            per = 2 * GRP + 3
            for g in range(NG):
                c0 = g * GRP
                act.wait_ge(s_a, 5 + per * g + 2 * GRP + 1)
                act.sqrt(sd[0:NP, c0:c0 + GRP], sd[0:NP, c0:c0 + GRP]).then_inc(s_sq, 1)
                act.wait_ge(s_a, 5 + per * (g + 1))
                for i in range(GRP):
                    col = h[0:NP, (c0 + i) * D:(c0 + i + 1) * D]
                    ins = act.activation(col, col, ACT.Relu, bias=nmr[0:NP, c0 + i:c0 + i + 1],
                                         scale=rstd[0:NP, c0 + i:c0 + i + 1])
                ins.then_inc(s_ac, 1)
                act.wait_ge(s_hT, g + 1)
                if g >= 2:
                    act.wait_ge(s_hp, g - 1)
                act.copy(colT[g % 2][:, 0:GRP * NP], ps[g % 2][:, 0:GRP * NP]).then_inc(s_hTc, 1)
            for b in range(NBT):
                act.wait_ge(s_segt, b + 2)
                t0, t1 = b * BT, min(b * BT + BT, TILES)
                act.copy(ncrel_all[:, t0:t1, :],
                         ps[b % 2][:, 0:(t1 - t0) * NS].rearrange("p (t s) -> p t s", s=NS)).then_inc(s_segc, 1)
            act.wait_ge(s_segc, NBT)

            def ids_of(s, q):
                if not isinstance(s, int) or s >= 2:
                    act.wait_ge(s_sel, (s - 1) * CHUNKS)
                    act.wait_ge(s_r, (s - 1) * 5)
                act.copy(ncrel[q][:], ncrel_all[:, :, bass.ds(s, 1)].rearrange("p t o -> p (t o)")).then_inc(s_ncr, 1)

            def select(v, q, cc):
                peel = isinstance(v, int)
                ts = chunk_tiles(cc)
                if cc == 0:
                    act.wait_ge(s_ncr, v + 1)
                if not peel or v * CHUNKS + cc >= 2:
                    act.wait_ge(s_sel, v * CHUNKS + cc - 1)
                par = (q * CHUNKS + cc) % 2
                for i, t in enumerate(ts):
                    act.activation(dist[par][:, i, :], iota[:], ACT.Abs, bias=ncrel[q][:, t:t + 1]).then_inc(s_dist, 1)
                act.wait_ge(s_dist, v * TILES + ts[-1] + 1)
                if not peel or v * CHUNKS + cc >= 3:
                    back = chunk_tiles((cc - 3) % CHUNKS)[-1] + 1 - (TILES if cc < 3 else 0)
                    act.wait_ge(s_agg, v * TILES + back)
                act.activation(sel[cc % 3][:, 0:len(ts), :], dist[par][:, 0:len(ts), :], ACT.Relu,
                               bias=1.0, scale=-1.0).then_inc(s_sel, 1)

            def attention(u, q, step):
                if step == 0:
                    act.wait_ge(s_add, (u + 1) * CHUNKS)
                    if not isinstance(u, int) or u >= 1:
                        act.wait_ge(s_lt, u)
                    act.copy(lc[:].rearrange("p (h t) -> p h t", h=HEADS),
                             G[q][:, :, D:TW].rearrange("p t h -> p h t")).then_inc(s_lc, 1)
                if step == 2:
                    act.wait_ge(s_mx, 5 * u + 5)
                    if not isinstance(u, int) or u >= 1:
                        act.wait_ge(s_pw, u)
                    act.activation(pt[:], dd[:], ACT.Exp).then_inc(s_exp, 1)
                if step == 3:
                    act.wait_ge(s_r, 5 * u + 3)
                    act.activation(rr[:], dr2[:], ACT.Exp).then_inc(s_rx, 1)

            def period(s, q, new=True, att=True, old=True, cur=True):
                for c in range(CHUNKS):
                    if c < LAG and old:
                        select(s - 2, q, c + CHUNKS - LAG)
                    if c >= LAG and cur:
                        select(s - 1, 1 - q, c - LAG)
                    if att and c < 4:
                        attention(s - 1, 1 - q, c)
                    if new and c == LAG:
                        ids_of(s, q)

            period(0, 0, att=False, old=False, cur=False)
            period(1, 1, old=False)
            with act.Fori(0, PAIRS) as k:
                period(k * 2 + 2, 0)
                period(k * 2 + 3, 1)
            if LEFT:
                period(NS - 1, (NS - 1) % 2)
            period(NS, NS % 2, new=False)
            period(NS + 1, (NS + 1) % 2, new=False, att=False, cur=False)
            perd = 3 * GRP + 3
            for g in range(NG):
                c0 = g * GRP
                act.wait_ge(s_yT, g + 1)
                if g >= 2:
                    act.wait_ge(s_o, g - 1)
                act.copy(colT[g % 2][:, 0:GRP * NP], ps[g % 2][:, 0:GRP * NP]).then_inc(s_yTc, 1)
                act.wait_ge(s_o, g + 1)
                if g >= 2:
                    act.wait_ge(s_res, 3 * (g - 1) - 2)
                act.activation(act_o[g % 2][0:NP, :], ps[2 + g % 2][0:NP, 0:GRP * D], ACT.Relu).then_inc(s_re, 1)
                act.wait_ge(s_dv, perd * g + 2 * GRP + 1)
                act.sqrt(sd[0:NP, c0:c0 + GRP], sd[0:NP, c0:c0 + GRP]).then_inc(s_sq, 1)


def arrange(x, src, dst, edge_attr_64, W_proj_w, W_proj_b, attn_vec, W_out_w, W_out_b, ln_gamma, ln_beta):
    import numpy as np

    E = src.shape[0]
    ns = E // SE
    padded = np.pad(dst, 1, constant_values=-1)
    t = lambda a: a.reshape(ns, TILES, P).transpose(0, 2, 1)
    meta = np.concatenate([t(src), t(dst), t(padded[:E])], axis=2)
    after = lambda n, k: padded[k::n][:E // n, None]
    win = np.concatenate([padded[:E].reshape(-1, P), after(P, P), after(P, P + 1)], axis=1).reshape(ns, 1, TILES, P + 2)
    seg = np.broadcast_to(win, (ns, HEADS, TILES, P + 2)).reshape(ns, GH, P + 2)
    dq = np.concatenate([padded[:E].reshape(ns, SE), after(SE, SE)], axis=1)
    ef = edge_attr_64.reshape(ns, SE, ED).transpose(0, 2, 1)
    row = lambda a: a.reshape(1, -1)
    named = dict(x=x, meta=meta, seg=seg, dq=dq, ef=ef, w_nat=W_proj_w, w_t=W_proj_w.T, b_proj=row(W_proj_b),
                 attn=attn_vec, wo_t=W_out_w.T, b_out=row(W_out_b), gamma=row(ln_gamma), beta=row(ln_beta))
    return {f"in_{k}": np.ascontiguousarray(v) for k, v in named.items()}


def kernel(**inputs):
    import numpy as np
    import concourse.bacc as bacc
    from concourse.bass_utils import run_bass_kernel_spmd

    ins = {k.replace("L0_gnn_", ""): np.asarray(v) for k, v in inputs.items()}
    arrays = arrange(**ins)
    nc = bacc.Bacc("TRN2", target_bir_lowering=False, num_devices=1)
    args = [nc.dram_tensor(k, a.shape, mybir.dt.from_np(a.dtype), kind="ExternalInput").ap() for k, a in arrays.items()]
    out = nc.dram_tensor("out_h", ins["x"].shape, F32, kind="ExternalOutput").ap()
    gnn_layer(nc, *args, out)
    return run_bass_kernel_spmd(nc, [arrays], core_ids=[0]).results[0]["out_h"]
```

```python
from contextlib import ExitStack

import concourse.bass as bass
from concourse import mybir

P = 128
HEADS = 4
D = 128
ED = 64
HD = D // HEADS
TW = D + HEADS
UW = TW + 1
TILES = 25
GH = HEADS * TILES
SE = TILES * P
CT = 3
CHUNKS = -(-TILES // CT)
LAG = 6
BIG = 1.0e30
EPS = 1e-5
UNROLL = 4
GRP = 4

ALU = mybir.AluOpType
ACT = mybir.ActivationFunctionType
F32 = mybir.dt.float32
I32 = mybir.dt.int32


def chunk_tiles(c):
    return range(c * CT, min(c * CT + CT, TILES))


def node_rows(n):
    return max(p for p in range(1, P + 1) if n % p == 0)


def gnn_layer(nc, x, meta, seg, dq, ef, w_nat, w_t, b_proj, attn, wo_t, b_out, gamma, beta, out):
    N = x.shape[0]
    NS = meta.shape[0]
    NP = node_rows(N)
    NC = N // NP
    assert 3 + UNROLL <= NS <= P and NC % GRP == 0
    NG = NC // GRP
    BLK = -(-min(N, NS * SE) // P)
    NT = NS * TILES
    TURNS = (NS - 3) // UNROLL
    LEFT = range(2 + TURNS * UNROLL, NS)

    with ExitStack() as ctx:
        def sb(name, shape, dt=F32):
            return ctx.enter_context(nc.sbuf_tensor(name, shape, dt))

        def sem(name):
            return ctx.enter_context(nc.semaphore(name))

        table = nc.dram_tensor("table_dram", (N, TW), F32, kind="Internal").ap()
        neigh = nc.dram_tensor("neigh_dram", (N, D), F32, kind="Internal").ap()
        boff_dram = nc.dram_tensor("boff_dram", (NS, TILES), I32, kind="Internal").ap()

        ps = [ctx.enter_context(nc.psum_tensor(f"ps{i}", [P, 512], F32)) for i in range(8)]
        e_ps = ps[0:2]
        agg_ps = ps[2:5]
        lt_ps, pw_ps, sm_ps = ps[5], ps[6], ps[7]

        UC = max((BLK + 1) * UW, NC * TW)
        U = sb("U", [P, UC])
        h = sb("h", [P, NC * D])
        WK = max(2 * TILES * UW + 2 * SE, 4 * SE + 1, NC * D)
        work = sb("work", [P, WK])
        G = [work[:, q * TILES * UW:(q + 1) * TILES * UW].rearrange("p (t w) -> p t w", w=UW) for q in range(2)]
        ef_sb = [work[0:ED, 2 * TILES * UW + q * SE:2 * TILES * UW + (q + 1) * SE] for q in range(2)]
        ncrel_all = sb("ncrel_all", [P, TILES, NS])
        boff = [sb(f"boff{q}", [1, TILES], I32) for q in range(2)]
        meta_sb = [sb(f"meta{q}", [P, 3 * TILES], I32) for q in range(2)]
        seg_sb = [sb(f"seg{q}", [GH, P + 2], I32) for q in range(2)]
        ncrel = [sb(f"ncrel{q}", [P, TILES]) for q in range(2)]
        started = sb("started", [P, TILES])
        ne = sb("ne", [GH, 2, P])
        cut = sb("cut", [GH, 2, P])
        cutmin = sb("cutmin", [GH, 2])
        lc = sb("lc", [P, GH])
        pre = sb("pre", [GH, P])
        suf = sb("suf", [GH, P])
        pre2 = sb("pre2", [GH, P])
        suf2 = sb("suf2", [GH, P])
        mx = sb("mx", [GH, P])
        dd = sb("dd", [GH, P])
        pt = sb("pt", [GH, P])
        ext = sb("ext", [1, 4, HEADS, TILES + 2])
        carry = sb("carry", [1, 2, 4 * (TILES + 2) + 4])
        ccomp = sb("ccomp", [1, 2 * GH])
        cinit = sb("cinit", [GH, 2])
        cont = sb("cont", [1, 1])
        hot = sb("hot", [1, P])
        dr = sb("dr", [1, HEADS])
        dr2 = sb("dr2", [1, HEADS])
        rr = sb("rr", [1, HEADS])
        r1 = sb("r1", [1, HEADS])
        fac = sb("fac", [P, HEADS])
        dist = [sb(f"dist{i}", [P, CT, 2 * P]) for i in range(2)]
        sel = [sb(f"sel{i}", [P, CT, 2 * P]) for i in range(3)]
        ident = sb("ident", [P, P])
        tri = sb("tri", [P, P])
        iota = sb("iota", [P, 2 * P])
        wx = sb("wx", [P, TW])
        we = sb("we", [ED, TW])
        wnat = sb("wnat", [P, D + ED])
        ablk = sb("ablk", [P, HEADS])
        bcol = sb("bcol", [P, 1])
        bwide = sb("bwide", [P, P])
        ones = sb("ones", [P, P])
        bias = sb("bias", [P, TW])
        wo = sb("wo", [P, D])
        bo = sb("bo", [1, D])
        gam = sb("gam", [P, D])
        bet = sb("bet", [P, D])
        stats = sb("stats", [P, GRP, 6])
        mv = sb("mv", [P, NC, 2])
        sd = sb("sd", [P, NC])
        rstd = sb("rstd", [P, NC])
        nmr = sb("nmr", [P, NC])
        colT = [sb(f"colT{i}", [P, GRP * P]) for i in range(2)]
        act_o = [sel[i][:].rearrange("p t n -> p (t n)")[:, 0:GRP * D] for i in range(2)]
        res = [dist[i][:].rearrange("p t n -> p (t n)")[:, 0:GRP * D] for i in range(2)]
        off = sb("off", [P, 1])
        cst = sb("cst", [P, TILES], I32)
        bint = sb("bint", [P, TILES], I32)
        boffs = sb("boffs", [P, TILES], I32)
        base = sb("base", [P, TILES])
        ids_flat = ncrel_all[:].rearrange("p t s -> p (t s)")
        LB = BLK * HEADS
        den = ids_flat[:, 0:LB] if TILES * NS >= 10 * BLK else sb("den", [P, LB])
        rden = ids_flat[:, LB:2 * LB] if TILES * NS >= 10 * BLK else sb("rden", [P, LB])
        empty = ids_flat[:, 2 * LB:2 * LB + BLK] if TILES * NS >= 10 * BLK else sb("empty", [P, BLK])
        rowf = ids_flat[:, 2 * LB + BLK:2 * LB + 2 * BLK] if TILES * NS >= 10 * BLK else sb("rowf", [P, BLK])
        rowi = sb("rowi", [P, BLK], I32)

        s_w = sem("s_w")
        s_blk = sem("s_blk")
        s_pass = {e: sem(f"s_pass{i}") for i, e in enumerate(
            (nc.sync.engine, nc.gpsimd.engine, nc.tensor.engine, nc.vector.engine))}
        s_const = sem("s_const")
        s_x = sem("s_x")
        s_dq = sem("s_dq")
        s_a = sem("s_a")
        s_aw = sem("s_aw")
        s_ac = sem("s_ac")
        s_hT = sem("s_hT")
        s_hTc = sem("s_hTc")
        s_hp = sem("s_hp")
        s_tab = sem("s_tab")
        s_tout = sem("s_tout")
        s_seg = sem("s_seg")
        s_segt = sem("s_segt")
        s_segc = sem("s_segc")
        s_boff = sem("s_boff")
        s_z = sem("s_z")
        s_u0 = sem("s_u0")
        s_meta = [sem(f"s_meta{q}") for q in range(2)]
        s_seg_in = [sem(f"s_seg_in{q}") for q in range(2)]
        s_off = [sem(f"s_off{q}") for q in range(2)]
        s_ef = [sem(f"s_ef{q}") for q in range(2)]
        s_gat = [[sem(f"s_gat{q}_{c}") for c in range(CHUNKS)] for q in range(2)]
        s_e = sem("s_e")
        s_add = sem("s_add")
        s_id = sem("s_id")
        s_cut = sem("s_cut")
        s_lc = sem("s_lc")
        s_lt = sem("s_lt")
        s_ncr = sem("s_ncr")
        s_sc1 = sem("s_sc1")
        s_smt = sem("s_smt")
        s_car = sem("s_car")
        s_cint = sem("s_cint")
        s_mx = sem("s_mx")
        s_exp = sem("s_exp")
        s_pw = sem("s_pw")
        s_pc = sem("s_pc")
        s_r = sem("s_r")
        s_rx = sem("s_rx")
        s_rf = sem("s_rf")
        s_f = sem("s_f")
        s_dist = sem("s_dist")
        s_sel = sem("s_sel")
        s_agg = sem("s_agg")
        s_acc = sem("s_acc")
        s_usc = sem("s_usc")
        s_n = sem("s_n")
        s_nb = sem("s_nb")
        s_sca = sem("s_sca")
        s_zin = sem("s_zin")
        s_y = sem("s_y")
        s_yT = sem("s_yT")
        s_yTc = sem("s_yTc")
        s_o = sem("s_o")
        s_re = sem("s_re")
        s_dv = sem("s_dv")
        s_sq = sem("s_sq")
        s_res = sem("s_res")
        s_out = [sem(f"s_out{i}") for i in range(2)]

        block = ctx.enter_context(nc.Block())

        x_cols = x.rearrange("(p c) d -> p (c d)", c=NC)
        out_cols = out.rearrange("(p c) d -> p (c d)", c=NC)
        XL = 5 if NC % 5 == 0 and (NC // 5) % GRP == 0 else 1
        XC = NC // XL
        WLOADS = 13
        dq_v = work[:, 0:SE + 1].bitcast(I32)
        st_v = work[:, SE + 1:2 * SE + 1]
        c_v = work[:, 2 * SE + 1:3 * SE + 1]
        nc_v = work[:, 3 * SE + 1:4 * SE + 1]
        BPT = 512 // NS if NS >= 8 else 4
        BT = min(BPT, 4)
        NBT = -(-TILES // BT)
        SB_STEPS = 9

        def settle(eng):
            eng.sem_inc(s_pass[eng.engine], 1)

        @block.sync
        def _(sp):
            for c in range(XL):
                sp.dma_start(h[0:NP, c * XC * D:(c + 1) * XC * D],
                             x_cols[:, c * XC * D:(c + 1) * XC * D]).then_inc(s_x, 16)
                sp.wait_ge(s_x, 16 * (c + 1))
                if c == 0:
                    sp.dma_start(wnat[:], w_nat).then_inc(s_w, 16)
                    sp.dma_start(wx[:, 0:D], w_t[0:D, :]).then_inc(s_w, 16)
                    sp.dma_start(we[:, 0:D], w_t[D:D + ED, :]).then_inc(s_w, 16)
                    sp.wait_ge(s_blk, 1)
                    for i in range(HEADS):
                        sp.dma_start(ablk[i * HD:(i + 1) * HD, i:i + 1],
                                     attn[i:i + 1, :].rearrange("a d -> d a")).then_inc(s_w, 16)
                    sp.dma_start(bcol[:], b_proj.rearrange("a d -> d a")).then_inc(s_w, 16)
                    sp.dma_start(bias[:, 0:D], b_proj.to_broadcast([P, D])).then_inc(s_w, 16)
                    sp.dma_start(wo[:], wo_t).then_inc(s_w, 16)
                    sp.dma_start(bo[:], b_out).then_inc(s_w, 16)
                    sp.dma_start(gam[:], gamma.to_broadcast([P, D])).then_inc(s_w, 16)
                    sp.dma_start(bet[:], beta.to_broadcast([P, D])).then_inc(s_w, 16)
                    sp.dma_start(dq_v[0:NS, :], dq).then_inc(s_dq, 16)
            sp.wait_ge(s_seg, 8)
            sp.dma_start(boff_dram, boffs[0:NS, :]).then_inc(s_boff, 16)
            sp.wait_ge(s_tab, NG)
            sp.dma_start(table.rearrange("(p c) w -> p (c w)", c=NC), U[0:NP, 0:NC * TW]).then_inc(s_tout, 16)
            sp.wait_ge(s_u0, 1)
            sp.dma_start(neigh.rearrange("(p c) d -> p (c d)", c=NC), U[0:NP, 0:NC * D]).then_inc(s_z, 16)

            def loads(s, q):
                peel = isinstance(s, int)
                if not peel or s >= 2:
                    sp.wait_ge(s_add, (s - 1) * CHUNKS)
                    settle(sp)
                    sp.wait_ge(s_id, (s - 1) * 2)
                settle(sp)
                sp.dma_start(meta_sb[q][:], meta[bass.ds(s, 1)].rearrange("o p m -> (o p) m")).then_inc(s_meta[q], 16)
                if not peel or s >= 2:
                    sp.wait_ge(s_e, (s - 1) * CHUNKS)
                settle(sp)
                sp.dma_start(ef_sb[q], ef[bass.ds(s, 1)].rearrange("o d e -> (o d) e")).then_inc(s_ef[q], 16)
                if not peel or s >= 2:
                    sp.wait_ge(s_acc, (s - 1) * TILES)
                if peel and s == 0:
                    sp.wait_ge(s_boff, 16)
                settle(sp)
                sp.dma_start(boff[q][:], boff_dram[bass.ds(s, 1), :]).then_inc(s_off[q], 16)
                if not peel or s >= 2:
                    sp.wait_ge(s_r, (s - 1) * 5)
                    settle(sp)
                    sp.wait_ge(s_cut, (s - 1) * 4)
                settle(sp)
                sp.dma_start(seg_sb[q][:], seg[bass.ds(s, 1)].rearrange("o r e -> (o r) e")).then_inc(s_seg_in[q], 16)

            sp.wait_ge(s_segt, 1 + NBT)
            loads(0, 0)
            loads(1, 1)
            with nc.Fori(0, TURNS, engines=(sp.engine,), hint_back_edge=True) as k:
                for j in range(UNROLL):
                    loads(k * UNROLL + 2 + j, j % 2)
            for s in LEFT:
                loads(s, s % 2)
            sp.wait_ge(s_agg, NT)
            sp.wait_ge(s_add, NS * CHUNKS)
            sp.dma_start(work[0:NP, 0:NC * D], x_cols).then_inc(s_x, 16)
            sp.wait_ge(s_sca, 16 * BLK)
            for c in range(XL):
                sp.dma_start(U[0:NP, c * XC * D:(c + 1) * XC * D],
                             neigh.rearrange("(p c) d -> p (c d)", c=NC)[:, c * XC * D:(c + 1) * XC * D]
                             ).then_inc(s_zin, 16)
                sp.wait_ge(s_zin, 16 * (c + 1))
            for g in range(NG):
                sp.wait_ge(s_res, 3 * (g + 1))
                sp.dma_start(out_cols[:, g * GRP * D:(g + 1) * GRP * D],
                             res[g % 2][0:NP, :]).then_inc(s_out[g % 2], 16)
            for i in range(2):
                sp.wait_ge(s_out[i], 16 * ((NG + 1 - i) // 2))

        @block.gpsimd
        def _(pool):
            pool.memset(ones[:], 1.0).then_inc(s_const, 1)
            pool.wait_ge(s_const, 1)
            pool.affine_select(out=ident[:], in_=ones[:], compare_op=ALU.is_equal, fill=0.0, base=0,
                               pattern=[[-1, P]], channel_multiplier=1).then_inc(s_const, 1)
            pool.affine_select(out=tri[:], in_=ones[:], compare_op=ALU.is_gt, fill=0.0, base=0,
                               pattern=[[1, P]], channel_multiplier=-1).then_inc(s_const, 1)
            pool.iota(iota[:], pattern=[[1, 2 * P]], base=0, channel_multiplier=0,
                      allow_small_or_imprecise_dtypes=True).then_inc(s_const, 1)
            pool.wait_ge(s_tout, 16)

            def gathers(s, q, turn):
                pool.wait_ge(s_meta[q], (turn + 1) * 16)
                for c in range(CHUNKS):
                    if not isinstance(s, int) or s >= 2:
                        pool.wait_ge(s_agg, (s - 2) * TILES + chunk_tiles(c)[-1] + 1)
                    settle(pool)
                    for t in chunk_tiles(c):
                        pool.indirect_dma_start(G[q][:, t, 0:TW], None, table,
                                                bass.IndirectOffsetOnAxis(ap=meta_sb[q][:, t:t + 1], axis=0)
                                                ).then_inc(s_gat[q][c], 16)

            gathers(0, 0, 0)
            gathers(1, 1, 0)
            with nc.Fori(0, TURNS, engines=(pool.engine,), hint_back_edge=True) as k:
                for j in range(UNROLL):
                    gathers(k * UNROLL + 2 + j, j % 2, k * (UNROLL // 2) + 1 + j // 2)
            for s in LEFT:
                gathers(s, s % 2, s // 2)
            pool.wait_ge(s_z, 16)
            for b in range(BLK):
                pool.wait_ge(s_nb, b + 1)
                pool.indirect_dma_start(neigh, bass.IndirectOffsetOnAxis(ap=rowi[:, b:b + 1], axis=0),
                                        U[:, b * UW:b * UW + D], None,
                                        bounds_check=N - 1, oob_is_err=False).then_inc(s_sca, 16)
            for c in range(XL):
                pool.wait_ge(s_zin, 16 * (c + 1))
                for g in range(c * XC // GRP, (c + 1) * XC // GRP):
                    a, e = g * GRP * D, (g + 1) * GRP * D
                    pool.tensor_tensor(h[0:NP, a:e], h[0:NP, a:e], U[0:NP, a:e], ALU.add).then_inc(s_y, 1)

        @block.tensor
        def _(pe):
            pe.wait_ge(s_const, 4)
            pe.wait_ge(s_w, 16 * WLOADS)
            pe.matmul(ps[7][:, 0:HEADS], wnat[:, 0:D], ablk[:], start=True, stop=True)
            pe.matmul(ps[7][0:ED, 4:4 + HEADS], wnat[:, D:D + ED], ablk[:], start=True, stop=True)
            pe.wait_ge(s_a, 2)
            pe.matmul(ps[7][:, 8:8 + HEADS], bwide[:], ablk[:], start=True, stop=True).then_inc(s_aw, 1)

            def turn_group(g, src, ready, value, done, free, freed):
                pe.wait_ge(ready, value)
                if g >= 2:
                    pe.wait_ge(free, freed)
                for i in range(GRP):
                    j = (g * GRP + i) * D
                    mm = pe.transpose(ps[g % 2][:, i * NP:(i + 1) * NP], src[0:NP, j:j + D], ident[0:NP, 0:NP])
                mm.then_inc(done, 1)

            def rows_group(g):
                pe.wait_ge(s_hTc, g + 1)
                if g == 0:
                    pe.wait_ge(s_a, 5)
                if g >= 2:
                    pe.wait_ge(s_tab, g - 1)
                for i in range(GRP):
                    bank = ps[2 + 2 * (g % 2) + i // 2]
                    mm = pe.matmul(bank[0:NP, (i % 2) * TW:(i % 2) * TW + TW],
                                   colT[g % 2][:, i * NP:(i + 1) * NP], wx[:], start=True, stop=True)
                mm.then_inc(s_hp, 1)

            for g in range(NG + 1):
                if g < NG:
                    turn_group(g, h, s_ac, g + 1, s_hT, s_hTc, g - 1)
                if g >= 1:
                    rows_group(g - 1)
            pe.wait_ge(s_seg, 2)
            pe.matmul(ps[6][0:NS, 0:1], tri[0:NS, 0:NS], c_v[0:NS, SE - 1:SE], start=True, stop=True).then_inc(s_segt, 1)
            pe.wait_ge(s_seg, SB_STEPS)
            for b in range(NBT):
                if b >= 2:
                    pe.wait_ge(s_segc, b - 1)
                if b < 2:
                    pe.wait_ge(s_hTc, NG)
                for i, t in enumerate(range(b * BT, min(b * BT + BT, TILES))):
                    mm = pe.transpose(ps[b % 2][:, i * NS:(i + 1) * NS], nc_v[0:NS, t * P:(t + 1) * P],
                                      ident[0:NS, 0:NS])
                mm.then_inc(s_segt, 1)
            pe.wait_ge(s_segc, NBT)
            pe.wait_ge(s_tab, NG)

            def edge_part(s, q, turn, c):
                peel = isinstance(s, int)
                if c == 0:
                    pe.wait_ge(s_ef[q], (turn + 1) * 16)
                if not peel or s * CHUNKS + c >= 2:
                    pe.wait_ge(s_add, s * CHUNKS + c - 1)
                bank = e_ps[(q * CHUNKS + c) % 2]
                for i, t in enumerate(chunk_tiles(c)):
                    mm = pe.matmul(bank[:, i * TW:(i + 1) * TW], ef_sb[q][:, t * P:(t + 1) * P], we[:],
                                   start=True, stop=True)
                mm.then_inc(s_e, 1)

            def attention(u, step):
                if step == 0:
                    pe.wait_ge(s_lc, u + 1)
                    if not isinstance(u, int) or u >= 1:
                        pe.wait_ge(s_mx, 5 * u)
                    pe.transpose(lt_ps[0:GH, 0:P], lc[:], ident[:]).then_inc(s_lt, 1)
                if step == 1:
                    pe.wait_ge(s_sc1, 2 * u + 2)
                    pe.wait_ge(s_cut, 4 * u + 4)
                    for i, col in enumerate((pre[:, P - 1:P], cutmin[:, 0:1], suf[:, 0:1], cutmin[:, 1:2])):
                        mm = pe.transpose(sm_ps[0:1, i * GH:(i + 1) * GH], col, ident[0:GH, 0:GH])
                    mm.then_inc(s_smt, 1)
                if step == 2:
                    pe.wait_ge(s_car, 4 * u + 4)
                    settle(pe)
                    for i in range(2):
                        mm = pe.transpose(sm_ps[0:GH, 400 + i:401 + i], ccomp[0:1, i * GH:(i + 1) * GH],
                                          ident[0:1, 0:1])
                    mm.then_inc(s_cint, 1)
                if step == 3:
                    pe.wait_ge(s_mx, 5 * u + 4)
                    pe.transpose(sm_ps[0:1, 0:GH], mx[:, 0:1], ident[0:GH, 0:GH])
                    pe.wait_ge(s_exp, u + 1)
                    if not isinstance(u, int) or u >= 1:
                        pe.wait_ge(s_f, CHUNKS * u)
                        pe.wait_ge(s_pc, u)
                    pe.transpose(pw_ps[:, 0:GH], pt[:], ident[0:GH, 0:GH]).then_inc(s_pw, 1)
                if step == 4:
                    pe.wait_ge(s_r, 5 * u + 5)
                    pe.matmul(sm_ps[:, 404:404 + HEADS], hot[0:1, :], r1[0:1, :], start=True, stop=True).then_inc(s_rf, 1)

            def sums(v, cc):
                pe.wait_ge(s_sel, v * CHUNKS + cc + 1)
                pe.wait_ge(s_f, v * CHUNKS + cc + 1)
                if cc == 0:
                    pe.wait_ge(s_pc, v + 1)
                    pe.wait_ge(s_id, v * 2 + 2)
                for t in chunk_tiles(cc):
                    back = 3 if t else 1
                    if not isinstance(v, int) or v * TILES + t >= 3:
                        pe.wait_ge(s_acc, v * TILES + t - back + 1)
                    for b in range(2):
                        mm = pe.matmul(agg_ps[t % 3][:, b * UW:(b + 1) * UW],
                                       sel[cc % 3][:, t - cc * CT, b * P:(b + 1) * P],
                                       G[pe_slot[0]][:, t, :], start=True, stop=True)
                    mm.then_inc(s_agg, 1)

            pe_slot = [0]

            def period(s, q, turn, new=True, att=True, old=True, cur=True, more=True):
                for c in range(CHUNKS):
                    if c < LAG and old:
                        pe_slot[0] = q
                        sums(s - 2, c + CHUNKS - LAG)
                    if c >= LAG and cur:
                        pe_slot[0] = 1 - q
                        sums(s - 1, c - LAG)
                    if new and c + 1 < CHUNKS:
                        edge_part(s, q, turn, c + 1)
                    if more and c + 1 == CHUNKS:
                        edge_part(s + 1, 1 - q, turn + q, 0)
                    if att and c in (0, 1, 2, 4, 5):
                        attention(s - 1, {0: 0, 1: 1, 2: 2, 4: 3, 5: 4}[c])

            edge_part(0, 0, 0, 0)
            period(0, 0, 0, att=False, old=False, cur=False)
            period(1, 1, 0, old=False)
            with nc.Fori(0, TURNS, engines=(pe.engine,), hint_back_edge=True) as k:
                for j in range(UNROLL):
                    period(k * UNROLL + 2 + j, j % 2, k * (UNROLL // 2) + 1 + j // 2)
            for s in LEFT:
                period(s, s % 2, s // 2, more=s + 1 < NS)
            period(NS, NS % 2, 0, new=False, more=False)
            period(NS + 1, (NS + 1) % 2, 0, new=False, att=False, cur=False, more=False)
            for g in range(NG + 1):
                if g < NG:
                    turn_group(g, h, s_y, g + 1, s_yT, s_yTc, g - 1)
                if g >= 1:
                    j = g - 1
                    pe.wait_ge(s_yTc, j + 1)
                    if j >= 2:
                        pe.wait_ge(s_re, j - 1)
                    for i in range(GRP):
                        o = ps[2 + j % 2][0:NP, i * D:(i + 1) * D]
                        pe.matmul(o, ones[0:1, 0:NP], bo[0:1, :], start=True, stop=False)
                        mm = pe.matmul(o, colT[j % 2][:, i * NP:(i + 1) * NP], wo[:], start=False, stop=True)
                    mm.then_inc(s_o, 1)

        @block.vector
        def _(dve):
            dve.memset(ablk[:], 0.0).then_inc(s_blk, 1)
            dve.wait_ge(s_w, 16 * WLOADS)
            dve.wait_ge(s_const, 4)
            dve.memset(rowi[:], 0).then_inc(s_a, 1)
            dve.tensor_scalar(bwide[:], ones[:], bcol[:, 0:1], None, ALU.mult).then_inc(s_a, 1)
            dve.wait_ge(s_aw, 1)
            dve.tensor_copy(wx[:, D:TW], ps[7][:, 0:HEADS]).then_inc(s_a, 1)
            dve.tensor_copy(we[:, D:TW], ps[7][0:ED, 4:4 + HEADS]).then_inc(s_a, 1)
            dve.tensor_copy(bias[:, D:TW], ps[7][:, 8:8 + HEADS]).then_inc(s_a, 1)
            dve.wait_ge(s_a, 5)

            def moments(g, src, cols, chain, n0):
                n = n0
                for i in range(GRP):
                    dve.bn_stats(stats[0:NP, i, :], src(i)).then_inc(chain, 1)
                n += GRP
                dve.wait_ge(chain, n)
                for i in range(GRP):
                    dve.bn_aggr(mv[0:NP, cols + i, :], stats[0:NP, i, :]).then_inc(chain, 1)
                n += GRP
                dve.wait_ge(chain, n)
                dve.tensor_scalar(sd[0:NP, cols:cols + GRP], mv[0:NP, cols:cols + GRP, 1], EPS, None,
                                  ALU.add).then_inc(chain, 1)
                return n + 1

            def inverse(cols, sq, value, chain, n):
                dve.wait_ge(sq, value)
                dve.reciprocal(rstd[0:NP, cols:cols + GRP], sd[0:NP, cols:cols + GRP]).then_inc(chain, 1)
                dve.wait_ge(chain, n + 1)
                dve.scalar_tensor_tensor(out=nmr[0:NP, cols:cols + GRP], in0=mv[0:NP, cols:cols + GRP, 0],
                                         scalar=-1.0, in1=rstd[0:NP, cols:cols + GRP],
                                         op0=ALU.mult, op1=ALU.mult).then_inc(chain, 1)
                return n + 2

            def store_rows(g):
                dve.wait_ge(s_hp, g + 1)
                for half in range(2):
                    bank = ps[2 + 2 * (g % 2) + half]
                    c0 = (g * GRP + 2 * half) * TW
                    ins = dve.tensor_tensor(
                        U[0:NP, c0:c0 + 2 * TW].rearrange("p (t w) -> p t w", w=TW),
                        bank[0:NP, 0:2 * TW].rearrange("p (t w) -> p t w", w=TW),
                        bias[0:NP, :].unsqueeze(1).to_broadcast([NP, 2, TW]), ALU.add)
                ins.then_inc(s_tab, 1)

            n = 5
            for g in range(NG):
                c0 = g * GRP
                dve.wait_ge(s_x, 16 * (c0 // XC + 1))
                n = moments(g, lambda i: h[0:NP, (c0 + i) * D:(c0 + i + 1) * D], c0, s_a, n)
                n = inverse(c0, s_sq, g + 1, s_a, n)
                if g >= 1:
                    store_rows(g - 1)
            store_rows(NG - 1)
            STEPS_A = n

            dve.wait_ge(s_dq, 16)
            dve.tensor_tensor(st_v[0:NS, :], dq_v[0:NS, 1:SE + 1], dq_v[0:NS, 0:SE], ALU.not_equal).then_inc(s_seg, 1)
            dve.wait_ge(s_seg, 1)
            dve.tensor_tensor_scan(c_v[0:NS, :], st_v[0:NS, :], st_v[0:NS, :], 0.0, ALU.add, ALU.max).then_inc(s_seg, 1)
            dve.wait_ge(s_segt, 1)
            dve.tensor_copy(off[0:NS, :], ps[6][0:NS, 0:1]).then_inc(s_seg, 1)
            dve.wait_ge(s_seg, 3)
            dve.tensor_scalar(c_v[0:NS, :], c_v[0:NS, :], off[0:NS, 0:1], -1.0, ALU.add, ALU.add).then_inc(s_seg, 1)
            dve.wait_ge(s_seg, 4)
            dve.tensor_copy(cst[0:NS, :], c_v[0:NS, 0:SE:P]).then_inc(s_seg, 1)
            dve.wait_ge(s_seg, 5)
            dve.tensor_scalar(bint[0:NS, :], cst[0:NS, :], 7, None, ALU.logical_shift_right).then_inc(s_seg, 1)
            dve.wait_ge(s_seg, 6)
            dve.tensor_scalar(base[0:NS, :], bint[0:NS, :], float(P), None, ALU.mult).then_inc(s_seg, 1)
            dve.tensor_scalar(boffs[0:NS, :], bint[0:NS, :], float(UW), None, ALU.mult).then_inc(s_seg, 1)
            dve.wait_ge(s_seg, 8)
            dve.tensor_tensor(nc_v[0:NS, :].rearrange("p (t e) -> p t e", e=P),
                              base[0:NS, :].unsqueeze(2).to_broadcast([NS, TILES, P]),
                              c_v[0:NS, :].rearrange("p (t e) -> p t e", e=P), ALU.subtract).then_inc(s_seg, 1)
            dve.wait_ge(s_tout, 16)
            dve.memset(U[:], 0.0).then_inc(s_u0, 1)
            dve.memset(ext[:], -BIG).then_inc(s_u0, 1)
            dve.wait_ge(s_segt, 1 + NBT)
            dve.wait_ge(s_u0, 2)

            def add_chunk(s, q, turn, c):
                ts = chunk_tiles(c)
                dve.wait_ge(s_gat[q][c], (turn + 1) * 16 * len(ts))
                dve.wait_ge(s_e, s * CHUNKS + c + 1)
                rows = G[q][:, ts[0]:ts[-1] + 1, 0:TW]
                dve.tensor_tensor(rows, rows,
                                  e_ps[(q * CHUNKS + c) % 2][:, 0:len(ts) * TW].rearrange("p (t w) -> p t w", w=TW),
                                  ALU.add).then_inc(s_add, 1)

            def node_ids(s, q):
                peel = isinstance(s, int)
                if not peel or s >= 1:
                    dve.wait_ge(s_id, 2 * s)
                cur, before = meta_sb[q][:, TILES:2 * TILES], meta_sb[q][:, 2 * TILES:3 * TILES]
                dve.tensor_tensor(started[:], cur, before, ALU.not_equal).then_inc(s_id, 1)
                if not peel or s >= 2:
                    dve.wait_ge(s_agg, (s - 1) * TILES)
                dve.wait_ge(s_id, 2 * s + 1)
                dve.tensor_tensor(G[q][:, :, UW - 1], started[:], cur, ALU.mult).then_inc(s_id, 1)

            def cuts(s, q, turn):
                dve.wait_ge(s_seg_in[q], (turn + 1) * 16)
                if not isinstance(s, int) or s >= 1:
                    dve.wait_ge(s_cut, 4 * s)
                    dve.wait_ge(s_mx, 5 * s)
                dve.tensor_tensor(ne[:, 0, :], seg_sb[q][:, 1:P + 1], seg_sb[q][:, 0:P], ALU.not_equal).then_inc(s_cut, 1)
                dve.tensor_tensor(ne[:, 1, :], seg_sb[q][:, 1:P + 1], seg_sb[q][:, 2:P + 2],
                                  ALU.not_equal).then_inc(s_cut, 1)
                dve.wait_ge(s_cut, 4 * s + 2)
                dve.tensor_scalar(cut[:], ne[:], -BIG, None, ALU.mult).then_inc(s_cut, 1)
                dve.wait_ge(s_cut, 4 * s + 3)
                dve.tensor_reduce(cutmin[:], cut[:], mybir.AxisListType.X, ALU.min).then_inc(s_cut, 1)

            EX = HEADS * (TILES + 2)

            flat = [ext[0:1, i].rearrange("o h t -> o (h t)") for i in range(4)]

            def scan(o, side, ini, chain):
                if side == 0:
                    dve.tensor_tensor_scan(o[:], cut[:, 0, :], lt_ps[0:GH, 0:P], ini, ALU.add, ALU.max).then_inc(chain, 1)
                else:
                    dve.tensor_tensor_scan(o[:, ::-1], cut[:, 1, ::-1], lt_ps[0:GH, 0:P][:, ::-1], ini,
                                           ALU.add, ALU.max).then_inc(chain, 1)

            def attention(u, q, c, part):
                later = not isinstance(u, int) or u >= 1
                if c == 1 and part == 0:
                    dve.wait_ge(s_lt, u + 1)
                    dve.wait_ge(s_cut, 4 * u + 4)
                    scan(pre, 0, -BIG, s_sc1)
                if c == 1 and part == 1:
                    scan(suf, 1, -BIG, s_sc1)
                if c == 2 and part == 0:
                    dve.wait_ge(s_smt, u + 1)
                    dve.tensor_copy(ext[0:1, :, :, 1:TILES + 1],
                                    sm_ps[0:1, 0:4 * GH].rearrange("o (k h t) -> o k h t", k=4, h=HEADS)
                                    ).then_inc(s_car, 1)
                if c == 2 and part == 1:
                    dve.wait_ge(s_car, 4 * u + 1)
                    if later:
                        dve.wait_ge(s_r, 5 * u)
                    dve.tensor_tensor_scan(carry[0:1, 0, 0:EX], flat[1], flat[0], -BIG, ALU.add, ALU.max).then_inc(s_car, 1)
                if c == 2 and part == 2:
                    dve.tensor_tensor_scan(carry_back[:, ::-1], flat[3][:, ::-1], flat[2][:, ::-1], -BIG,
                                           ALU.add, ALU.max).then_inc(s_car, 1)
                if c == 2 and part == 3:
                    dve.wait_ge(s_car, 4 * u + 3)
                    dve.tensor_copy(ccomp[0:1, :].rearrange("o (k h t) -> o k h t", k=2, h=HEADS),
                                    carry_view).then_inc(s_car, 1)
                if c == 3 and part == 0:
                    dve.wait_ge(s_cint, u + 1)
                    dve.tensor_copy(cinit[:], sm_ps[0:GH, 400:402]).then_inc(s_mx, 1)
                if c == 3 and part == 1:
                    dve.wait_ge(s_mx, 5 * u + 1)
                    scan(pre2, 0, cinit[:, 0:1], s_mx)
                if c == 3 and part == 2:
                    scan(suf2, 1, cinit[:, 1:2], s_mx)
                if c == 3 and part == 3:
                    dve.wait_ge(s_mx, 5 * u + 3)
                    dve.tensor_tensor(mx[:], pre2[:], suf2[:], ALU.max).then_inc(s_mx, 1)
                if c == 3 and part == 4:
                    dve.wait_ge(s_mx, 5 * u + 4)
                    if later:
                        dve.wait_ge(s_exp, u)
                    dve.tensor_tensor(dd[:], lt_ps[0:GH, 0:P], mx[:], ALU.subtract).then_inc(s_mx, 1)
                    dve.wait_ge(s_ncr, u + 1)
                    if later:
                        dve.wait_ge(s_rf, u)
                    dve.tensor_scalar(hot[:], iota[0:1, 0:P], ncrel[q][0:1, 0:1], 0.0, ALU.add, ALU.is_equal)
                    dve.tensor_tensor(cont[:], seg_sb[q][0:1, 1:2], seg_sb[q][0:1, 0:1], ALU.is_equal).then_inc(s_r, 1)
                if c == 5 and part == 0:
                    dve.wait_ge(s_pw, u + 1)
                    dve.wait_ge(s_add, (u + 1) * CHUNKS)
                    dve.wait_ge(s_lc, u + 1)
                    dve.tensor_copy(G[q][:, :, D:TW],
                                    pw_ps[:, 0:GH].rearrange("p (h t) -> p t h", h=HEADS)).then_inc(s_pc, 1)
                    dve.tensor_tensor(dr[:], carry[0:1, 0, 0:EX:TILES + 2], sm_ps[0:1, 0:GH:TILES],
                                      ALU.subtract).then_inc(s_r, 1)
                if c == 5 and part == 1:
                    dve.wait_ge(s_r, 5 * u + 2)
                    dve.tensor_scalar(dr2[:], dr[:], cont[0:1, 0:1], None, ALU.mult).then_inc(s_r, 1)
                    dve.tensor_copy(ext[0:1, 0, :, 0], carry[0:1, 0, TILES:EX:TILES + 2]).then_inc(s_r, 1)
                if c == 5 and part == 4:
                    dve.wait_ge(s_rx, u + 1)
                    dve.tensor_scalar(r1[:], rr[:], -1.0, None, ALU.add).then_inc(s_r, 1)

            carry_back = carry[:].rearrange("o k x -> o (k x)")[:, EX + 2:2 * EX + 2]
            carry_view = carry[:, :, 0:EX].rearrange("o k (h p) -> o k h p", h=HEADS)[:, :, :, 0:TILES]

            def rescale(u, off0):
                dve.wait_ge(s_rf, u + 1)
                dve.tensor_scalar(fac[:], sm_ps[:, 404:404 + HEADS], 1.0, None, ALU.add).then_inc(s_usc, 1)
                dve.wait_ge(s_usc, 3 * u + 1)
                if not isinstance(u, int) or u >= 1:
                    dve.wait_ge(s_acc, TILES * u)
                num = U[:, bass.ds(off0, D)].rearrange("p (h d) -> p h d", h=HEADS)
                dve.tensor_tensor(num, num, fac[:].unsqueeze(2).to_broadcast([P, HEADS, HD]), ALU.mult).then_inc(s_usc, 1)
                dn = U[:, bass.ds(off0 + D, HEADS)]
                dve.tensor_tensor(dn, dn, fac[:], ALU.mult).then_inc(s_usc, 1)

            def weight(q, c):
                ts = chunk_tiles(c)
                rows = G[q][:, ts[0]:ts[-1] + 1, 0:D].rearrange("p t (h d) -> p t h d", h=HEADS)
                w = pw_ps[:, 0:GH].rearrange("p (h t) -> p t h", h=HEADS)[:, ts[0]:ts[-1] + 1, :]
                dve.tensor_tensor(rows, rows, w.unsqueeze(3).to_broadcast([P, len(ts), HEADS, HD]),
                                  ALU.mult).then_inc(s_f, 1)

            def offsets(q, turn):
                dve.wait_ge(s_off[q], (turn + 1) * 16)
                settle(dve)
                return nc.values_load_multi_w_load_instructions(
                    boff[q][0:1, 0:TILES], engines=[dve.engine], min_val=0,
                    max_val=(BLK - 1) * UW,
                    skip_runtime_bounds_check_because="compact ids are below the number of nodes")[1]

            def accumulate(v, t, offs):
                dve.wait_ge(s_agg, v * TILES + t + 1)
                if t == 0:
                    dve.wait_ge(s_usc, 3 * v + 3)
                if not isinstance(v, int) or v * TILES + t >= 1:
                    dve.wait_ge(s_acc, v * TILES + t)
                two = U[:, bass.ds(offs[t], 2 * UW)]
                dve.tensor_tensor(two, two, agg_ps[t % 3][:, 0:2 * UW], ALU.add).then_inc(s_acc, 1)

            def period(s, q, turn, offs, new=True, att=True, old=True, cur=True):
                if old and offs is None:
                    offs = offsets(q, turn - 1)
                for c in range(CHUNKS):
                    v, tiles = None, []
                    if c < LAG and old:
                        v, tiles = s - 2, chunk_tiles(c + CHUNKS - LAG)
                    if c == LAG and cur:
                        offs = offsets(1 - q, turn - 1 + q)
                        rescale(s - 1, offs[0])
                    if c >= LAG and cur:
                        v, tiles = s - 1, chunk_tiles(c - LAG)
                    if len(tiles) > 0:
                        accumulate(v, tiles[0], offs)
                    if att:
                        attention(s - 1, 1 - q, c, 0)
                    if c + 1 < LAG and old:
                        weight(q, c + 1 + CHUNKS - LAG)
                    if c + 1 >= LAG and cur:
                        weight(1 - q, c + 1 - LAG)
                    if att:
                        attention(s - 1, 1 - q, c, 1)
                    if len(tiles) > 1:
                        accumulate(v, tiles[1], offs)
                    if att:
                        attention(s - 1, 1 - q, c, 2)
                    if new:
                        add_chunk(s, q, turn, c)
                    if att:
                        attention(s - 1, 1 - q, c, 3)
                    if len(tiles) > 2:
                        accumulate(v, tiles[2], offs)
                    if att:
                        attention(s - 1, 1 - q, c, 4)
                    if new and c == 5:
                        node_ids(s, q)
                    if new and c == 6:
                        cuts(s, q, turn)
                return offs

            period(0, 0, 0, None, att=False, old=False, cur=False)
            period(1, 1, 0, None, old=False)
            with nc.Fori(0, TURNS, engines=(dve.engine,), hint_back_edge=True) as k:
                for j in range(UNROLL):
                    offs = period(k * UNROLL + 2 + j, j % 2, k * (UNROLL // 2) + 1 + j // 2, offs if j else None)
            for i, s in enumerate(LEFT):
                offs = period(s, s % 2, s // 2, offs if i else None)
            offs = period(NS, NS % 2, NS // 2, offs, new=False)
            period(NS + 1, (NS + 1) % 2, (NS + 1) // 2, offs, new=False, att=False, cur=False)

            dve.wait_ge(s_acc, NT)
            ub = U[:, 0:BLK * UW].rearrange("p (b w) -> p b w", w=UW)
            den3 = den[:].rearrange("p (b h) -> p b h", h=HEADS)
            rden3 = rden[:].rearrange("p (b h) -> p b h", h=HEADS)
            dve.tensor_scalar(den3, ub[:, :, D:TW], 1.0 / BIG, None, ALU.max).then_inc(s_n, 1)
            dve.tensor_scalar(empty[:], ub[:, :, D], 0.0, float(4 * N), ALU.is_equal, ALU.mult).then_inc(s_n, 1)
            dve.wait_ge(s_n, 2)
            dve.reciprocal(rden[:], den[:]).then_inc(s_n, 1)
            dve.tensor_tensor(rowf[:], empty[:], ub[:, :, UW - 1], ALU.add).then_inc(s_n, 1)
            dve.wait_ge(s_n, 4)
            dve.tensor_copy(rowi[:], rowf[:]).then_inc(s_n, 1)
            dve.wait_ge(s_n, 5)
            for b in range(BLK):
                num = ub[:, b, 0:D].rearrange("p (h d) -> p h d", h=HEADS)
                dve.tensor_tensor(num, num, rden3[:, b, :].unsqueeze(2).to_broadcast([P, HEADS, HD]),
                                  ALU.mult).then_inc(s_nb, 1)
            dve.wait_ge(s_x, 16 * (XL + 1))
            n = 0
            for g in range(NG):
                c0 = g * GRP
                dve.wait_ge(s_re, g + 1)
                n = moments(g, lambda i: act_o[g % 2][0:NP, i * D:(i + 1) * D], c0, s_dv, n)
                n = inverse(c0, s_sq, NG + g + 1, s_dv, n)
                dve.wait_ge(s_dv, n)
                if g >= 2:
                    dve.wait_ge(s_out[g % 2], 16 * (g // 2))
                for i in range(GRP):
                    dve.tensor_scalar(act_o[g % 2][0:NP, i * D:(i + 1) * D], act_o[g % 2][0:NP, i * D:(i + 1) * D],
                                      rstd[0:NP, c0 + i:c0 + i + 1], nmr[0:NP, c0 + i:c0 + i + 1],
                                      ALU.mult, ALU.add).then_inc(s_dv, 1)
                n += GRP
                dve.wait_ge(s_dv, n)
                r3 = res[g % 2][0:NP, :].rearrange("p (t d) -> p t d", d=D)
                a3 = act_o[g % 2][0:NP, :].rearrange("p (t d) -> p t d", d=D)
                dve.tensor_tensor(r3, a3, gam[0:NP, :].unsqueeze(1).to_broadcast([NP, GRP, D]), ALU.mult).then_inc(s_res, 1)
                dve.wait_ge(s_res, 3 * g + 1)
                dve.tensor_tensor(r3, r3, bet[0:NP, :].unsqueeze(1).to_broadcast([NP, GRP, D]), ALU.add).then_inc(s_res, 1)
                dve.wait_ge(s_res, 3 * g + 2)
                dve.tensor_tensor(res[g % 2][0:NP, :], res[g % 2][0:NP, :],
                                  work[0:NP, c0 * D:(c0 + GRP) * D], ALU.add).then_inc(s_res, 1)

        @block.scalar
        def _(act):
            per = 2 * GRP + 3
            for g in range(NG):
                c0 = g * GRP
                act.wait_ge(s_a, 5 + per * g + 2 * GRP + 1)
                act.sqrt(sd[0:NP, c0:c0 + GRP], sd[0:NP, c0:c0 + GRP]).then_inc(s_sq, 1)
                act.wait_ge(s_a, 5 + per * (g + 1))
                for i in range(GRP):
                    col = h[0:NP, (c0 + i) * D:(c0 + i + 1) * D]
                    ins = act.activation(col, col, ACT.Relu, bias=nmr[0:NP, c0 + i:c0 + i + 1],
                                         scale=rstd[0:NP, c0 + i:c0 + i + 1])
                ins.then_inc(s_ac, 1)
                act.wait_ge(s_hT, g + 1)
                if g >= 2:
                    act.wait_ge(s_hp, g - 1)
                act.copy(colT[g % 2][:, 0:GRP * NP], ps[g % 2][:, 0:GRP * NP]).then_inc(s_hTc, 1)
            for b in range(NBT):
                act.wait_ge(s_segt, b + 2)
                t0, t1 = b * BT, min(b * BT + BT, TILES)
                act.copy(ncrel_all[:, t0:t1, :],
                         ps[b % 2][:, 0:(t1 - t0) * NS].rearrange("p (t s) -> p t s", s=NS)).then_inc(s_segc, 1)
            act.wait_ge(s_segc, NBT)

            def ids_of(s, q):
                if not isinstance(s, int) or s >= 2:
                    act.wait_ge(s_sel, (s - 1) * CHUNKS)
                    act.wait_ge(s_r, (s - 1) * 5)
                act.copy(ncrel[q][:], ncrel_all[:, :, bass.ds(s, 1)].rearrange("p t o -> p (t o)")).then_inc(s_ncr, 1)

            def select(v, q, cc):
                peel = isinstance(v, int)
                ts = chunk_tiles(cc)
                if cc == 0:
                    act.wait_ge(s_ncr, v + 1)
                if not peel or v * CHUNKS + cc >= 2:
                    act.wait_ge(s_sel, v * CHUNKS + cc - 1)
                par = (q * CHUNKS + cc) % 2
                for i, t in enumerate(ts):
                    act.activation(dist[par][:, i, :], iota[:], ACT.Abs, bias=ncrel[q][:, t:t + 1]).then_inc(s_dist, 1)
                act.wait_ge(s_dist, v * TILES + ts[-1] + 1)
                if not peel or v * CHUNKS + cc >= 3:
                    back = chunk_tiles((cc - 3) % CHUNKS)[-1] + 1 - (TILES if cc < 3 else 0)
                    act.wait_ge(s_agg, v * TILES + back)
                act.activation(sel[cc % 3][:, 0:len(ts), :], dist[par][:, 0:len(ts), :], ACT.Relu,
                               bias=1.0, scale=-1.0).then_inc(s_sel, 1)

            def attention(u, q, step):
                if step == 0:
                    act.wait_ge(s_add, (u + 1) * CHUNKS)
                    if not isinstance(u, int) or u >= 1:
                        act.wait_ge(s_lt, u)
                    act.copy(lc[:].rearrange("p (h t) -> p h t", h=HEADS),
                             G[q][:, :, D:TW].rearrange("p t h -> p h t")).then_inc(s_lc, 1)
                if step == 2:
                    act.wait_ge(s_mx, 5 * u + 5)
                    if not isinstance(u, int) or u >= 1:
                        act.wait_ge(s_pw, u)
                    act.activation(pt[:], dd[:], ACT.Exp).then_inc(s_exp, 1)
                if step == 3:
                    act.wait_ge(s_r, 5 * u + 3)
                    act.activation(rr[:], dr2[:], ACT.Exp).then_inc(s_rx, 1)

            def period(s, q, new=True, att=True, old=True, cur=True):
                for c in range(CHUNKS):
                    if c + 2 < LAG and old:
                        select(s - 2, q, c + 2 + CHUNKS - LAG)
                    if c + 2 >= LAG and cur:
                        select(s - 1, 1 - q, c + 2 - LAG)
                    if att and c in (0, 4, 5):
                        attention(s - 1, 1 - q, {0: 0, 4: 2, 5: 3}[c])
                    if new and c == LAG:
                        ids_of(s, q)

            period(0, 0, att=False, old=False, cur=False)
            period(1, 1, old=False)
            with nc.Fori(0, TURNS, engines=(act.engine,), hint_back_edge=True) as k:
                for j in range(UNROLL):
                    period(k * UNROLL + 2 + j, j % 2)
            for s in LEFT:
                period(s, s % 2)
            period(NS, NS % 2, new=False)
            period(NS + 1, (NS + 1) % 2, new=False, att=False, cur=False)
            perd = 3 * GRP + 3
            for g in range(NG):
                c0 = g * GRP
                act.wait_ge(s_yT, g + 1)
                if g >= 2:
                    act.wait_ge(s_o, g - 1)
                act.copy(colT[g % 2][:, 0:GRP * NP], ps[g % 2][:, 0:GRP * NP]).then_inc(s_yTc, 1)
                act.wait_ge(s_o, g + 1)
                if g >= 2:
                    act.wait_ge(s_res, 3 * (g - 1) - 2)
                act.activation(act_o[g % 2][0:NP, :], ps[2 + g % 2][0:NP, 0:GRP * D], ACT.Relu).then_inc(s_re, 1)
                act.wait_ge(s_dv, perd * g + 2 * GRP + 1)
                act.sqrt(sd[0:NP, c0:c0 + GRP], sd[0:NP, c0:c0 + GRP]).then_inc(s_sq, 1)


def arrange(x, src, dst, edge_attr_64, W_proj_w, W_proj_b, attn_vec, W_out_w, W_out_b, ln_gamma, ln_beta):
    import numpy as np

    E = src.shape[0]
    ns = E // SE
    padded = np.pad(dst, 1, constant_values=-1)
    t = lambda a: a.reshape(ns, TILES, P).transpose(0, 2, 1)
    meta = np.concatenate([t(src), t(dst), t(padded[:E])], axis=2)
    after = lambda n, k: padded[k::n][:E // n, None]
    win = np.concatenate([padded[:E].reshape(-1, P), after(P, P), after(P, P + 1)], axis=1).reshape(ns, 1, TILES, P + 2)
    seg = np.broadcast_to(win, (ns, HEADS, TILES, P + 2)).reshape(ns, GH, P + 2)
    dq = np.concatenate([padded[:E].reshape(ns, SE), after(SE, SE)], axis=1)
    ef = edge_attr_64.reshape(ns, SE, ED).transpose(0, 2, 1)
    row = lambda a: a.reshape(1, -1)
    named = dict(x=x, meta=meta, seg=seg, dq=dq, ef=ef, w_nat=W_proj_w, w_t=W_proj_w.T, b_proj=row(W_proj_b),
                 attn=attn_vec, wo_t=W_out_w.T, b_out=row(W_out_b), gamma=row(ln_gamma), beta=row(ln_beta))
    return {f"in_{k}": np.ascontiguousarray(v) for k, v in named.items()}


def kernel(**inputs):
    import numpy as np
    import concourse.bacc as bacc
    from concourse.bass_utils import run_bass_kernel_spmd

    ins = {k.replace("L0_gnn_", ""): np.asarray(v) for k, v in inputs.items()}
    arrays = arrange(**ins)
    nc = bacc.Bacc("TRN2", target_bir_lowering=False, num_devices=1)
    args = [nc.dram_tensor(k, a.shape, mybir.dt.from_np(a.dtype), kind="ExternalInput").ap() for k, a in arrays.items()]
    out = nc.dram_tensor("out_h", ins["x"].shape, F32, kind="ExternalOutput").ap()
    gnn_layer(nc, *args, out)
    return run_bass_kernel_spmd(nc, [arrays], core_ids=[0]).results[0]["out_h"]
```

```python
from contextlib import ExitStack

import concourse.bass as bass
from concourse import mybir

P = 128
HEADS = 4
D = 128
ED = 64
HD = D // HEADS
TW = D + HEADS
UW = TW + 1
TILES = 25
GH = HEADS * TILES
SE = TILES * P
CT = 3
CHUNKS = -(-TILES // CT)
LAG = 6
BIG = 1.0e30
EPS = 1e-5
UNROLL = 4
GRP = 4

ALU = mybir.AluOpType
ACT = mybir.ActivationFunctionType
F32 = mybir.dt.float32
I32 = mybir.dt.int32


def chunk_tiles(c):
    return range(c * CT, min(c * CT + CT, TILES))


def gnn_layer(nc, x, meta, seg, dq, ef, w_nat, w_t, b_proj, attn, wo_t, b_out, gamma, beta, out):
    N = x.shape[0]
    NS = meta.shape[0]
    NC = -(-N // P)
    FULL = N // P
    assert 3 + UNROLL <= NS <= P and NC > GRP
    NG = -(-NC // GRP)
    BLK = -(-min(N, NS * SE) // P)
    NT = NS * TILES
    TURNS = (NS - 3) // UNROLL
    LEFT = range(2 + TURNS * UNROLL, NS)

    with ExitStack() as ctx:
        def sb(name, shape, dt=F32):
            return ctx.enter_context(nc.sbuf_tensor(name, shape, dt))

        def sem(name):
            return ctx.enter_context(nc.semaphore(name))

        table = nc.dram_tensor("table_dram", (NC * P, TW), F32, kind="Internal").ap()
        neigh = nc.dram_tensor("neigh_dram", (NC * P, D), F32, kind="Internal").ap()
        boff_dram = nc.dram_tensor("boff_dram", (NS, TILES), I32, kind="Internal").ap()

        ps = [ctx.enter_context(nc.psum_tensor(f"ps{i}", [P, 512], F32)) for i in range(8)]
        e_ps = ps[0:2]
        agg_ps = ps[2:5]
        lt_ps, pw_ps, sm_ps = ps[5], ps[6], ps[7]

        UC = max((BLK + 1) * UW, NC * TW)
        U = sb("U", [P, UC])
        h = sb("h", [P, NC * D])
        WK = max(2 * TILES * UW + 2 * SE, 4 * SE + 1, NC * D)
        work = sb("work", [P, WK])
        G = [work[:, q * TILES * UW:(q + 1) * TILES * UW].rearrange("p (t w) -> p t w", w=UW) for q in range(2)]
        ef_sb = [work[0:ED, 2 * TILES * UW + q * SE:2 * TILES * UW + (q + 1) * SE] for q in range(2)]
        ncrel_all = sb("ncrel_all", [P, TILES, NS])
        boff = [sb(f"boff{q}", [1, TILES], I32) for q in range(2)]
        meta_sb = [sb(f"meta{q}", [P, 3 * TILES], I32) for q in range(2)]
        seg_sb = [sb(f"seg{q}", [GH, P + 2], I32) for q in range(2)]
        ncrel = [sb(f"ncrel{q}", [P, TILES]) for q in range(2)]
        started = sb("started", [P, TILES])
        ne = sb("ne", [GH, 2, P])
        cut = sb("cut", [GH, 2, P])
        cutmin = sb("cutmin", [GH, 2])
        lc = sb("lc", [P, GH])
        pre = sb("pre", [GH, P])
        suf = sb("suf", [GH, P])
        pre2 = sb("pre2", [GH, P])
        suf2 = sb("suf2", [GH, P])
        mx = sb("mx", [GH, P])
        dd = sb("dd", [GH, P])
        pt = sb("pt", [GH, P])
        ext = sb("ext", [1, 4, HEADS, TILES + 2])
        carry = sb("carry", [1, 2, 4 * (TILES + 2) + 4])
        ccomp = sb("ccomp", [1, 2 * GH])
        cinit = sb("cinit", [GH, 2])
        cont = sb("cont", [1, 1])
        hot = sb("hot", [1, P])
        dr = sb("dr", [1, HEADS])
        dr2 = sb("dr2", [1, HEADS])
        rr = sb("rr", [1, HEADS])
        r1 = sb("r1", [1, HEADS])
        fac = sb("fac", [P, HEADS])
        selmem = sb("selmem", [P, 5 * CT * 2 * P])
        mats = [selmem[:, i * CT * 2 * P:(i + 1) * CT * 2 * P].rearrange("p (t n) -> p t n", n=2 * P) for i in range(5)]
        dist, sel = mats[0:2], mats[2:5]
        ident = sb("ident", [P, P])
        tri = sb("tri", [P, P])
        iota = sb("iota", [P, 2 * P])
        wx = sb("wx", [P, TW])
        we = sb("we", [ED, TW])
        wnat = sb("wnat", [P, D + ED])
        ablk = sb("ablk", [P, HEADS])
        bcol = sb("bcol", [P, 1])
        bwide = sb("bwide", [P, P])
        ones = sb("ones", [P, P])
        bias = sb("bias", [P, TW])
        wo = sb("wo", [P, D])
        bo = sb("bo", [1, D])
        gam = sb("gam", [P, D])
        bet = sb("bet", [P, D])
        stats = sb("stats", [P, 2, GRP, 6])
        mv = sb("mv", [P, NC, 2])
        sd = sb("sd", [P, NC])
        rstd = sb("rstd", [P, NC])
        nmr = sb("nmr", [P, NC])
        eps = sb("eps", [P, 1])
        colT = [sb(f"colT{i}", [P, GRP * P]) for i in range(2)]
        act_o = [selmem[:, i * GRP * D:(i + 1) * GRP * D] for i in range(4)]
        res = [selmem[:, i * GRP * D:(i + 1) * GRP * D] for i in range(4, 7)]
        off = sb("off", [P, 1])
        cst = sb("cst", [P, TILES], I32)
        bint = sb("bint", [P, TILES], I32)
        boffs = sb("boffs", [P, TILES], I32)
        base = sb("base", [P, TILES])
        ids_flat = ncrel_all[:].rearrange("p t s -> p (t s)")
        LB = BLK * HEADS
        den = ids_flat[:, 0:LB] if TILES * NS >= 10 * BLK else sb("den", [P, LB])
        rden = ids_flat[:, LB:2 * LB] if TILES * NS >= 10 * BLK else sb("rden", [P, LB])
        empty = ids_flat[:, 2 * LB:2 * LB + BLK] if TILES * NS >= 10 * BLK else sb("empty", [P, BLK])
        rowf = ids_flat[:, 2 * LB + BLK:2 * LB + 2 * BLK] if TILES * NS >= 10 * BLK else sb("rowf", [P, BLK])
        rowi = sb("rowi", [P, BLK], I32)

        s_w = sem("s_w")
        s_wd = sem("s_wd")
        s_blk = sem("s_blk")
        s_pass = {e: sem(f"s_pass{i}") for i, e in enumerate(
            (nc.sync.engine, nc.gpsimd.engine, nc.tensor.engine, nc.vector.engine))}
        s_const = sem("s_const")
        s_dq = sem("s_dq")
        s_wc = sem("s_wc")
        s_aw = sem("s_aw")
        s_h0 = sem("s_h0")
        s_st = sem("s_st")
        s_sq = sem("s_sq")
        s_nm = sem("s_nm")
        s_ac = sem("s_ac")
        s_hT = sem("s_hT")
        s_hTc = sem("s_hTc")
        s_hp = sem("s_hp")
        s_tab = sem("s_tab")
        s_tout = sem("s_tout")
        s_first = sem("s_first")
        s_seg = sem("s_seg")
        s_rel = sem("s_rel")
        s_segt = sem("s_segt")
        s_segc = sem("s_segc")
        s_boff = sem("s_boff")
        s_z = sem("s_z")
        s_u0 = sem("s_u0")
        s_meta = [sem(f"s_meta{q}") for q in range(2)]
        s_seg_in = [sem(f"s_seg_in{q}") for q in range(2)]
        s_off = [sem(f"s_off{q}") for q in range(2)]
        s_ef = [sem(f"s_ef{q}") for q in range(2)]
        s_gat = [[sem(f"s_gat{q}_{c}") for c in range(CHUNKS)] for q in range(2)]
        s_e = sem("s_e")
        s_add = sem("s_add")
        s_id = sem("s_id")
        s_cut = sem("s_cut")
        s_lc = sem("s_lc")
        s_lt = sem("s_lt")
        s_ncr = sem("s_ncr")
        s_sc1 = sem("s_sc1")
        s_smt = sem("s_smt")
        s_car = sem("s_car")
        s_cint = sem("s_cint")
        s_mx = sem("s_mx")
        s_exp = sem("s_exp")
        s_pw = sem("s_pw")
        s_pc = sem("s_pc")
        s_r = sem("s_r")
        s_rx = sem("s_rx")
        s_rf = sem("s_rf")
        s_f = sem("s_f")
        s_dist = sem("s_dist")
        s_sel = sem("s_sel")
        s_agg = sem("s_agg")
        s_acc = sem("s_acc")
        s_usc = sem("s_usc")
        s_n = sem("s_n")
        s_nb = sem("s_nb")
        s_w0 = sem("s_w0")
        s_xd = sem("s_xd")
        s_sca = [sem(f"s_sca{i}") for i in range(4)]
        s_zin = [sem(f"s_zin{i}") for i in range(4)]
        s_yT = sem("s_yT")
        s_yTc = sem("s_yTc")
        s_o = sem("s_o")
        s_re = sem("s_re")
        s_dst = sem("s_dst")
        s_dsq = sem("s_dsq")
        s_dnm = sem("s_dnm")
        s_norm = sem("s_norm")
        s_res = sem("s_res")
        s_out = [sem(f"s_out{i}") for i in range(3)]

        block = ctx.enter_context(nc.Block())

        def cols_of(dram, c0, c1):
            return dram[c0 * P:c1 * P, :].rearrange("(c p) d -> p c d", p=P)

        def cols_in(sbuf, c0, c1, w=D):
            return sbuf[:, c0 * w:c1 * w].rearrange("p (c d) -> p c d", d=w)

        def group(g):
            return g * GRP, min(GRP, NC - g * GRP)

        x_cuts = [0] + list(range(GRP, max(NC - 4 * GRP, GRP + 1), 5 * GRP)) + [NC]
        x_piece = [max(i for i in range(len(x_cuts) - 1) if x_cuts[i] <= g * GRP) for g in range(NG)]
        s_x = [sem(f"s_x{i}") for i in range(len(x_cuts) - 1)]
        t_cuts = sorted(set(range(0, NG, 5)) | {NG - 1, NG})
        WLOADS = 9
        dq_v = work[:, 0:SE + 1].bitcast(I32)
        st_v = work[:, SE + 1:2 * SE + 1]
        c_v = work[:, 2 * SE + 1:3 * SE + 1]
        nc_v = work[:, 3 * SE + 1:4 * SE + 1]
        BT = min(512 // NS, 4)
        NBT = -(-TILES // BT)
        SCAN_SLOT, BASE_SLOT, IDS_SLOT = 2, 5, 8
        SLOTS = max(NG + 4, IDS_SLOT + NBT + 1)

        def load_nodes(eng, dst, c0, c1, arrived):
            if min(c1, FULL) > c0:
                eng.dma_start(cols_in(dst, c0, min(c1, FULL)), cols_of(x, c0, min(c1, FULL))).then_inc(arrived, 16)
            if c1 > FULL:
                eng.dma_start(dst[0:N - FULL * P, FULL * D:NC * D], x[FULL * P:N, :]).then_inc(arrived, 16)

        def count_nodes(c0, c1):
            return (min(c1, FULL) > c0) + (c1 > FULL)

        def scattered(g):
            return sum(max(0, min(GRP, BLK - GRP * i)) for i in range(g % 4, g + 1, 4))

        def settle(eng):
            eng.sem_inc(s_pass[eng.engine], 1)

        @block.sync
        def _(sp):
            for i in range(len(x_cuts) - 1):
                if x_cuts[i + 1] == NC:
                    sp.wait_ge(s_h0, 1)
                load_nodes(sp, h, x_cuts[i], x_cuts[i + 1], s_x[i])
                if i == 1:
                    sp.wait_ge(s_w, 16 * WLOADS)
                    sp.dma_start(dq_v[0:NS, :], dq).then_inc(s_dq, 16)

            def loads(s, q):
                peel = isinstance(s, int)
                if not peel or s >= 2:
                    sp.wait_ge(s_add, (s - 1) * CHUNKS)
                    settle(sp)
                    sp.wait_ge(s_id, (s - 1) * 2)
                settle(sp)
                sp.dma_start(meta_sb[q][:], meta[bass.ds(s, 1)].rearrange("o p m -> (o p) m")).then_inc(s_meta[q], 16)
                if not peel or s >= 2:
                    sp.wait_ge(s_e, (s - 1) * CHUNKS)
                settle(sp)
                sp.dma_start(ef_sb[q], ef[bass.ds(s, 1)].rearrange("o d e -> (o d) e")).then_inc(s_ef[q], 16)
                if not peel or s >= 2:
                    sp.wait_ge(s_acc, (s - 1) * TILES)
                if peel and s == 0:
                    sp.wait_ge(s_boff, 16)
                settle(sp)
                sp.dma_start(boff[q][:], boff_dram[bass.ds(s, 1), :]).then_inc(s_off[q], 16)
                if not peel or s >= 2:
                    sp.wait_ge(s_r, (s - 1) * 5)
                    settle(sp)
                    sp.wait_ge(s_cut, (s - 1) * 4)
                settle(sp)
                sp.dma_start(seg_sb[q][:], seg[bass.ds(s, 1)].rearrange("o r e -> (o r) e")).then_inc(s_seg_in[q], 16)

            sp.wait_ge(s_seg, 6)
            sp.dma_start(boff_dram, boffs[0:NS, :]).then_inc(s_boff, 16)
            for g0, g1 in zip(t_cuts, t_cuts[1:]):
                sp.wait_ge(s_tab, g1)
                c0, c1 = g0 * GRP, min(g1 * GRP, NC)
                sp.dma_start(cols_of(table, c0, c1), cols_in(U, c0, c1, TW)).then_inc(s_tout, 16)
            sp.wait_ge(s_segt, 1 + NBT)
            loads(0, 0)
            loads(1, 1)
            sp.wait_ge(s_u0, 1)
            sp.dma_start(cols_of(neigh, 0, NC), cols_in(U, 0, NC)).then_inc(s_z, 16)
            with nc.Fori(0, TURNS, engines=(sp.engine,), hint_back_edge=True) as k:
                for j in range(UNROLL):
                    loads(k * UNROLL + 2 + j, j % 2)
            for s in LEFT:
                loads(s, s % 2)
            sp.wait_ge(s_agg, NT)
            sp.wait_ge(s_add, NS * CHUNKS)
            load_nodes(sp, work, 0, FULL, s_xd)
            if NC > FULL:
                sp.wait_ge(s_w0, 1)
                load_nodes(sp, work, FULL, NC, s_xd)
            STORE_LAG = 6
            for g in range(NG + STORE_LAG):
                if g < NG:
                    if g * GRP < BLK:
                        sp.wait_ge(s_sca[g % 4], 16 * scattered(g))
                    if g >= 4:
                        sp.wait_ge(s_yT, g - 3)
                    c0, k = group(g)
                    sp.dma_start(cols_in(U, c0, c0 + k), cols_of(neigh, c0, c0 + k)).then_inc(s_zin[g % 4], 16)
                if g >= STORE_LAG:
                    j = g - STORE_LAG
                    c0, k = group(j)
                    sp.wait_ge(s_res, 3 * (j + 1))
                    full = min(k, FULL - c0)
                    if full > 0:
                        sp.dma_start(cols_of(out, c0, c0 + full), cols_in(res[j % 3], 0, full)).then_inc(s_out[j % 3], 16)
                    if full < k:
                        sp.dma_start(out[FULL * P:N, :],
                                     res[j % 3][0:N - FULL * P, full * D:k * D]).then_inc(s_out[j % 3], 16)
            for i in range(3):
                sp.wait_ge(s_out[i], 16 * sum(count_nodes(group(j)[0], sum(group(j))) for j in range(i, NG, 3)))

        @block.gpsimd
        def _(pool):
            pool.memset(ones[:], 1.0).then_inc(s_const, 1)
            pool.wait_ge(s_const, 1)
            pool.affine_select(out=ident[:], in_=ones[:], compare_op=ALU.is_equal, fill=0.0, base=0,
                               pattern=[[-1, P]], channel_multiplier=1).then_inc(s_const, 1)
            pool.affine_select(out=tri[:], in_=ones[:], compare_op=ALU.is_gt, fill=0.0, base=0,
                               pattern=[[1, P]], channel_multiplier=-1).then_inc(s_const, 1)
            pool.iota(iota[:], pattern=[[1, 2 * P]], base=0, channel_multiplier=0,
                      allow_small_or_imprecise_dtypes=True).then_inc(s_const, 1)
            pool.wait_ge(s_seg, 7)
            pool.tensor_tensor(nc_v[0:NS, :].rearrange("p (t e) -> p t e", e=P),
                               base[0:NS, :].unsqueeze(2).to_broadcast([NS, TILES, P]),
                               c_v[0:NS, :].rearrange("p (t e) -> p t e", e=P), ALU.subtract).then_inc(s_rel, 1)
            pool.wait_ge(s_segt, 1 + NBT)
            pool.wait_ge(s_tout, 16 * (len(t_cuts) - 1))

            def gathers(s, q, turn):
                pool.wait_ge(s_meta[q], (turn + 1) * 16)
                for c in range(CHUNKS):
                    if not isinstance(s, int) or s >= 2:
                        pool.wait_ge(s_agg, (s - 2) * TILES + chunk_tiles(c)[-1] + 1)
                    settle(pool)
                    for t in chunk_tiles(c):
                        pool.indirect_dma_start(G[q][:, t, 0:TW], None, table,
                                                bass.IndirectOffsetOnAxis(ap=meta_sb[q][:, t:t + 1], axis=0)
                                                ).then_inc(s_gat[q][c], 16)

            gathers(0, 0, 0)
            gathers(1, 1, 0)
            with nc.Fori(0, TURNS, engines=(pool.engine,), hint_back_edge=True) as k:
                for j in range(UNROLL):
                    gathers(k * UNROLL + 2 + j, j % 2, k * (UNROLL // 2) + 1 + j // 2)
            for s in LEFT:
                gathers(s, s % 2, s // 2)
            pool.wait_ge(s_z, 16)
            for b in range(BLK):
                g = b // GRP
                if b % GRP == 0 and g >= 4:
                    pool.wait_ge(s_sca[g % 4], 16 * scattered(g - 4))
                pool.wait_ge(s_nb, b + 1)
                pool.indirect_dma_start(neigh, bass.IndirectOffsetOnAxis(ap=rowi[:, b:b + 1], axis=0),
                                        U[:, b * UW:b * UW + D], None,
                                        bounds_check=N - 1, oob_is_err=False).then_inc(s_sca[g % 4], 16)

        @block.tensor
        def _(pe):
            pe.wait_ge(s_const, 4)
            pe.wait_ge(s_w, 16 * WLOADS)
            pe.matmul(ps[7][:, 0:HEADS], wnat[:, 0:D], ablk[:], start=True, stop=True)
            pe.matmul(ps[7][0:ED, 4:4 + HEADS], wnat[:, D:D + ED], ablk[:], start=True, stop=True)
            pe.wait_ge(s_wc, 2)
            pe.matmul(ps[7][:, 8:8 + HEADS], bwide[:], ablk[:], start=True, stop=True).then_inc(s_aw, 1)

            def transposes(g):
                c0, k = group(g)
                pe.wait_ge(s_ac, g + 1)
                if g >= 2:
                    pe.wait_ge(s_hTc, g - 1)
                for i in range(k):
                    mm = pe.transpose(ps[g % 2][:, i * P:(i + 1) * P], h[:, (c0 + i) * D:(c0 + i + 1) * D], ident[:])
                mm.then_inc(s_hT, 1)

            def table_rows(g):
                pe.wait_ge(s_hTc, g + 1)
                if g == 0:
                    pe.wait_ge(s_wc, 5)
                if g >= 2:
                    pe.wait_ge(s_tab, g - 1)
                for i in range(group(g)[1]):
                    bank = ps[2 + 2 * (g % 2) + i // 2]
                    mm = pe.matmul(bank[:, (i % 2) * TW:(i % 2) * TW + TW],
                                   colT[g % 2][:, i * P:(i + 1) * P], wx[:], start=True, stop=True)
                mm.then_inc(s_hp, 1)

            for sl in range(SLOTS):
                if 3 <= sl < NG + 3:
                    table_rows(sl - 3)
                if 1 <= sl <= NG:
                    transposes(sl - 1)
                if sl == SCAN_SLOT + 1:
                    pe.wait_ge(s_seg, 1)
                    pe.wait_ge(s_wc, 5)
                    pe.matmul(ps[6][0:NS, 0:1], tri[0:NS, 0:NS], c_v[0:NS, SE - 1:SE], start=True,
                              stop=True).then_inc(s_segt, 1)
                b = sl - IDS_SLOT
                if 0 <= b < NBT:
                    if b == 0:
                        pe.wait_ge(s_rel, 1)
                    if b >= 2:
                        pe.wait_ge(s_segc, b - 1)
                    for i, t in enumerate(range(b * BT, min(b * BT + BT, TILES))):
                        mm = pe.transpose(ps[6 + b % 2][:, i * NS:(i + 1) * NS], nc_v[0:NS, t * P:(t + 1) * P],
                                          ident[0:NS, 0:NS])
                    mm.then_inc(s_segt, 1)
            pe.wait_ge(s_segc, NBT)
            pe.wait_ge(s_tab, NG)

            def edge_part(s, q, turn, c):
                peel = isinstance(s, int)
                if c == 0:
                    pe.wait_ge(s_ef[q], (turn + 1) * 16)
                if not peel or s * CHUNKS + c >= 2:
                    pe.wait_ge(s_add, s * CHUNKS + c - 1)
                bank = e_ps[(q * CHUNKS + c) % 2]
                for i, t in enumerate(chunk_tiles(c)):
                    mm = pe.matmul(bank[:, i * TW:(i + 1) * TW], ef_sb[q][:, t * P:(t + 1) * P], we[:],
                                   start=True, stop=True)
                mm.then_inc(s_e, 1)

            def attention(u, c):
                if c == 0:
                    pe.wait_ge(s_lc, u + 1)
                    if not isinstance(u, int) or u >= 1:
                        pe.wait_ge(s_mx, 5 * u)
                    pe.transpose(lt_ps[0:GH, 0:P], lc[:], ident[:]).then_inc(s_lt, 1)
                if c == 1:
                    pe.wait_ge(s_sc1, 2 * u + 2)
                    pe.wait_ge(s_cut, 4 * u + 4)
                    for i, col in enumerate((pre[:, P - 1:P], cutmin[:, 0:1], suf[:, 0:1], cutmin[:, 1:2])):
                        mm = pe.transpose(sm_ps[0:1, i * GH:(i + 1) * GH], col, ident[0:GH, 0:GH])
                    mm.then_inc(s_smt, 1)
                if c == 2:
                    pe.wait_ge(s_car, 4 * u + 4)
                    settle(pe)
                    for i in range(2):
                        mm = pe.transpose(sm_ps[0:GH, 400 + i:401 + i], ccomp[0:1, i * GH:(i + 1) * GH],
                                          ident[0:1, 0:1])
                    mm.then_inc(s_cint, 1)
                if c == 4:
                    pe.wait_ge(s_mx, 5 * u + 4)
                    pe.transpose(sm_ps[0:1, 0:GH], mx[:, 0:1], ident[0:GH, 0:GH])
                    pe.wait_ge(s_exp, u + 1)
                    if not isinstance(u, int) or u >= 1:
                        pe.wait_ge(s_f, CHUNKS * u)
                        pe.wait_ge(s_pc, u)
                    pe.transpose(pw_ps[:, 0:GH], pt[:], ident[0:GH, 0:GH]).then_inc(s_pw, 1)
                if c == 5:
                    pe.wait_ge(s_r, 5 * u + 5)
                    pe.matmul(sm_ps[:, 404:404 + HEADS], hot[0:1, :], r1[0:1, :], start=True, stop=True).then_inc(s_rf, 1)

            def sums(v, q, cc):
                pe.wait_ge(s_sel, v * CHUNKS + cc + 1)
                pe.wait_ge(s_f, v * CHUNKS + cc + 1)
                if cc == 0:
                    pe.wait_ge(s_pc, v + 1)
                    pe.wait_ge(s_id, v * 2 + 2)
                for t in chunk_tiles(cc):
                    back = 3 if t else 1
                    if not isinstance(v, int) or v * TILES + t >= 3:
                        pe.wait_ge(s_acc, v * TILES + t - back + 1)
                    for b in range(2):
                        mm = pe.matmul(agg_ps[t % 3][:, b * UW:(b + 1) * UW],
                                       sel[cc % 3][:, t - cc * CT, b * P:(b + 1) * P],
                                       G[q][:, t, :], start=True, stop=True)
                    mm.then_inc(s_agg, 1)

            def period(s, q, turn, new=True, att=True, old=True, cur=True, more=True):
                for c in range(CHUNKS):
                    if c < LAG and old:
                        sums(s - 2, q, c + CHUNKS - LAG)
                    if c >= LAG and cur:
                        sums(s - 1, 1 - q, c - LAG)
                    if new and c + 1 < CHUNKS:
                        edge_part(s, q, turn, c + 1)
                    if more and c + 1 == CHUNKS:
                        edge_part(s + 1, 1 - q, turn + q, 0)
                    if att:
                        attention(s - 1, c)

            edge_part(0, 0, 0, 0)
            period(0, 0, 0, att=False, old=False, cur=False)
            period(1, 1, 0, old=False)
            with nc.Fori(0, TURNS, engines=(pe.engine,), hint_back_edge=True) as k:
                for j in range(UNROLL):
                    period(k * UNROLL + 2 + j, j % 2, k * (UNROLL // 2) + 1 + j // 2)
            for s in LEFT:
                period(s, s % 2, s // 2, more=s + 1 < NS)
            period(NS, NS % 2, 0, new=False, more=False)
            period(NS + 1, (NS + 1) % 2, 0, new=False, att=False, cur=False, more=False)
            pe.wait_ge(s_wd, 16 * 4)
            for g in range(NG + 1):
                if g < NG:
                    c0, k = group(g)
                    pe.wait_ge(s_zin[g % 4], 16 * (g // 4 + 1))
                    if g >= 2:
                        pe.wait_ge(s_yTc, g - 1)
                    for i in range(k):
                        yT, cols = ps[g % 2][:, i * P:(i + 1) * P], slice((c0 + i) * D, (c0 + i + 1) * D)
                        pe.matmul(yT, h[:, cols], ident[:], start=True, stop=False)
                        mm = pe.matmul(yT, U[:, cols], ident[:], start=False, stop=True)
                    mm.then_inc(s_yT, 1)
                if g >= 1:
                    j = g - 1
                    pe.wait_ge(s_yTc, j + 1)
                    if j >= 2:
                        pe.wait_ge(s_re, j - 1)
                    for i in range(group(j)[1]):
                        o = ps[2 + j % 2][:, i * D:(i + 1) * D]
                        pe.matmul(o, ones[0:1, :], bo[0:1, :], start=True, stop=False)
                        mm = pe.matmul(o, colT[j % 2][:, i * P:(i + 1) * P], wo[:], start=False, stop=True)
                    mm.then_inc(s_o, 1)

        @block.vector
        def _(dve):
            dve.memset(ablk[:], 0.0).then_inc(s_blk, 1)
            dve.memset(eps[:], EPS)
            dve.memset(h[:, (NC - 1) * D:NC * D], 0.0).then_inc(s_h0, 1)

            def weight_columns(step):
                if step == 0:
                    dve.wait_ge(s_w, 16 * WLOADS)
                    dve.wait_ge(s_const, 4)
                    dve.memset(rowi[:], 0).then_inc(s_wc, 1)
                    dve.tensor_scalar(bwide[:], ones[:], bcol[:, 0:1], None, ALU.mult).then_inc(s_wc, 1)
                if step == 1:
                    dve.wait_ge(s_aw, 1)
                    dve.tensor_copy(wx[:, D:TW], ps[7][:, 0:HEADS]).then_inc(s_wc, 1)
                    dve.tensor_copy(we[:, D:TW], ps[7][0:ED, 4:4 + HEADS]).then_inc(s_wc, 1)
                    dve.tensor_copy(bias[:, D:TW], ps[7][:, 8:8 + HEADS]).then_inc(s_wc, 1)
                    dve.wait_ge(s_wc, 5)

            def bn_stats(g, src, done):
                for i in range(group(g)[1]):
                    ins = dve.bn_stats(stats[:, g % 2, i, :], src[:, i * D:(i + 1) * D])
                ins.then_inc(done, 1)

            def bn_aggr(g, done):
                c0, k = group(g)
                dve.wait_ge(done, 2 * g + 1)
                for i in range(k):
                    ins = dve.bn_aggr(mv[:, c0 + i, :], stats[:, g % 2, i, :])
                ins.then_inc(done, 1)

            def inverse(g, sqrt_done, done):
                c0, k = group(g)
                dve.wait_ge(sqrt_done, g + 1)
                dve.reciprocal(rstd[:, c0:c0 + k], sd[:, c0:c0 + k]).then_inc(done, 1)

            def minus_mean(g, done):
                c0, k = group(g)
                dve.wait_ge(done, 2 * g + 1)
                dve.scalar_tensor_tensor(out=nmr[:, c0:c0 + k], in0=mv[:, c0:c0 + k, 0], scalar=-1.0,
                                         in1=rstd[:, c0:c0 + k], op0=ALU.mult, op1=ALU.mult).then_inc(done, 1)

            def store_rows(g):
                dve.wait_ge(s_hp, g + 1)
                c0, k = group(g)
                for i in range(0, k, 2):
                    n = min(2, k - i)
                    ins = dve.tensor_tensor(
                        cols_in(U, c0 + i, c0 + i + n, TW),
                        ps[2 + 2 * (g % 2) + i // 2][:, 0:n * TW].rearrange("p (t w) -> p t w", w=TW),
                        bias[:].unsqueeze(1).to_broadcast([P, n, TW]), ALU.add)
                ins.then_inc(s_tab, 1)

            def block_offsets():
                dve.wait_ge(s_segt, 1)
                dve.tensor_copy(off[0:NS, :], ps[6][0:NS, 0:1]).then_inc(s_seg, 1)
                dve.wait_ge(s_seg, 2)
                dve.tensor_scalar(base[0:NS, :], c_v[0:NS, 0:SE:P], off[0:NS, 0:1], -1.0, ALU.add, ALU.add).then_inc(s_seg, 1)
                dve.wait_ge(s_seg, 3)
                dve.tensor_copy(cst[0:NS, :], base[0:NS, :]).then_inc(s_seg, 1)
                dve.wait_ge(s_seg, 4)
                dve.tensor_scalar(bint[0:NS, :], cst[0:NS, :], 7, None, ALU.logical_shift_right).then_inc(s_seg, 1)
                dve.wait_ge(s_seg, 5)
                dve.tensor_scalar(base[0:NS, :], bint[0:NS, :], float(P), None, ALU.mult)
                dve.tensor_scalar(boffs[0:NS, :], bint[0:NS, :], float(UW), None, ALU.mult).then_inc(s_seg, 1)
                dve.wait_ge(s_seg, 6)
                dve.tensor_scalar(base[0:NS, :], base[0:NS, :], off[0:NS, 0:1], 1.0, ALU.subtract, ALU.add).then_inc(s_seg, 1)

            for sl in range(SLOTS):
                if sl < NG:
                    c0, k = group(sl)
                    i = x_piece[sl]
                    dve.wait_ge(s_x[i], 16 * count_nodes(x_cuts[i], x_cuts[i + 1]))
                    bn_stats(sl, h[:, c0 * D:(c0 + k) * D], s_st)
                if 1 <= sl <= NG:
                    inverse(sl - 1, s_sq, s_nm)
                if sl < NG:
                    bn_aggr(sl, s_st)
                if 1 <= sl <= NG:
                    minus_mean(sl - 1, s_nm)
                if sl in (0, 1):
                    weight_columns(sl)
                if 4 <= sl < NG + 4:
                    store_rows(sl - 4)
                if sl == SCAN_SLOT - 1:
                    dve.wait_ge(s_dq, 16)
                    dve.tensor_tensor(st_v[0:NS, :], dq_v[0:NS, 1:SE + 1], dq_v[0:NS, 0:SE],
                                      ALU.not_equal).then_inc(s_first, 1)
                if sl == SCAN_SLOT:
                    dve.wait_ge(s_first, 1)
                    dve.tensor_tensor_scan(c_v[0:NS, :], st_v[0:NS, :], st_v[0:NS, :], 0.0, ALU.add, ALU.max).then_inc(s_seg, 1)
                if sl == BASE_SLOT:
                    block_offsets()
            dve.wait_ge(s_tout, 16 * (len(t_cuts) - 1))
            dve.memset(U[:], 0.0).then_inc(s_u0, 1)
            dve.memset(ext[:], -BIG).then_inc(s_u0, 1)
            dve.wait_ge(s_segt, 1 + NBT)
            dve.wait_ge(s_u0, 2)

            def add_chunk(s, q, turn, c):
                ts = chunk_tiles(c)
                dve.wait_ge(s_gat[q][c], (turn + 1) * 16 * len(ts))
                dve.wait_ge(s_e, s * CHUNKS + c + 1)
                rows = G[q][:, ts[0]:ts[-1] + 1, 0:TW]
                dve.tensor_tensor(rows, rows,
                                  e_ps[(q * CHUNKS + c) % 2][:, 0:len(ts) * TW].rearrange("p (t w) -> p t w", w=TW),
                                  ALU.add).then_inc(s_add, 1)

            def node_ids(s, q):
                peel = isinstance(s, int)
                if not peel or s >= 1:
                    dve.wait_ge(s_id, 2 * s)
                cur, before = meta_sb[q][:, TILES:2 * TILES], meta_sb[q][:, 2 * TILES:3 * TILES]
                dve.tensor_tensor(started[:], cur, before, ALU.not_equal).then_inc(s_id, 1)
                if not peel or s >= 2:
                    dve.wait_ge(s_agg, (s - 1) * TILES)
                dve.wait_ge(s_id, 2 * s + 1)
                dve.tensor_tensor(G[q][:, :, UW - 1], started[:], cur, ALU.mult).then_inc(s_id, 1)

            def cuts(s, q, turn):
                dve.wait_ge(s_seg_in[q], (turn + 1) * 16)
                if not isinstance(s, int) or s >= 1:
                    dve.wait_ge(s_cut, 4 * s)
                    dve.wait_ge(s_mx, 5 * s)
                dve.tensor_tensor(ne[:, 0, :], seg_sb[q][:, 1:P + 1], seg_sb[q][:, 0:P], ALU.not_equal).then_inc(s_cut, 1)
                dve.tensor_tensor(ne[:, 1, :], seg_sb[q][:, 1:P + 1], seg_sb[q][:, 2:P + 2],
                                  ALU.not_equal).then_inc(s_cut, 1)
                dve.wait_ge(s_cut, 4 * s + 2)
                dve.tensor_scalar(cut[:], ne[:], -BIG, None, ALU.mult).then_inc(s_cut, 1)
                dve.wait_ge(s_cut, 4 * s + 3)
                dve.tensor_reduce(cutmin[:], cut[:], mybir.AxisListType.X, ALU.min).then_inc(s_cut, 1)

            EX = HEADS * (TILES + 2)

            flat = [ext[0:1, i].rearrange("o h t -> o (h t)") for i in range(4)]

            def scan(o, side, ini, chain):
                if side == 0:
                    dve.tensor_tensor_scan(o[:], cut[:, 0, :], lt_ps[0:GH, 0:P], ini, ALU.add, ALU.max).then_inc(chain, 1)
                else:
                    dve.tensor_tensor_scan(o[:, ::-1], cut[:, 1, ::-1], lt_ps[0:GH, 0:P][:, ::-1], ini,
                                           ALU.add, ALU.max).then_inc(chain, 1)

            def attention(u, q, c, part):
                later = not isinstance(u, int) or u >= 1
                if c == 1 and part == 0:
                    dve.wait_ge(s_lt, u + 1)
                    dve.wait_ge(s_cut, 4 * u + 4)
                    scan(pre, 0, -BIG, s_sc1)
                if c == 1 and part == 1:
                    scan(suf, 1, -BIG, s_sc1)
                if c == 2 and part == 0:
                    dve.wait_ge(s_smt, u + 1)
                    dve.tensor_copy(ext[0:1, :, :, 1:TILES + 1],
                                    sm_ps[0:1, 0:4 * GH].rearrange("o (k h t) -> o k h t", k=4, h=HEADS)
                                    ).then_inc(s_car, 1)
                if c == 2 and part == 1:
                    dve.wait_ge(s_car, 4 * u + 1)
                    if later:
                        dve.wait_ge(s_r, 5 * u)
                    dve.tensor_tensor_scan(carry[0:1, 0, 0:EX], flat[1], flat[0], -BIG, ALU.add, ALU.max).then_inc(s_car, 1)
                if c == 2 and part == 2:
                    dve.tensor_tensor_scan(carry_back[:, ::-1], flat[3][:, ::-1], flat[2][:, ::-1], -BIG,
                                           ALU.add, ALU.max).then_inc(s_car, 1)
                if c == 2 and part == 3:
                    dve.wait_ge(s_car, 4 * u + 3)
                    dve.tensor_copy(ccomp[0:1, :].rearrange("o (k h t) -> o k h t", k=2, h=HEADS),
                                    carry_view).then_inc(s_car, 1)
                if c == 3 and part == 0:
                    dve.wait_ge(s_cint, u + 1)
                    dve.tensor_copy(cinit[:], sm_ps[0:GH, 400:402]).then_inc(s_mx, 1)
                if c == 3 and part == 1:
                    dve.wait_ge(s_mx, 5 * u + 1)
                    scan(pre2, 0, cinit[:, 0:1], s_mx)
                if c == 3 and part == 2:
                    scan(suf2, 1, cinit[:, 1:2], s_mx)
                if c == 3 and part == 3:
                    dve.wait_ge(s_mx, 5 * u + 3)
                    dve.tensor_tensor(mx[:], pre2[:], suf2[:], ALU.max).then_inc(s_mx, 1)
                if c == 3 and part == 4:
                    dve.wait_ge(s_mx, 5 * u + 4)
                    if later:
                        dve.wait_ge(s_exp, u)
                    dve.tensor_tensor(dd[:], lt_ps[0:GH, 0:P], mx[:], ALU.subtract).then_inc(s_mx, 1)
                    dve.wait_ge(s_ncr, u + 1)
                    if later:
                        dve.wait_ge(s_rf, u)
                    dve.tensor_scalar(hot[:], iota[0:1, 0:P], ncrel[q][0:1, 0:1], 0.0, ALU.add, ALU.is_equal)
                    dve.tensor_tensor(cont[:], seg_sb[q][0:1, 1:2], seg_sb[q][0:1, 0:1], ALU.is_equal).then_inc(s_r, 1)
                if c == 5 and part == 0:
                    dve.wait_ge(s_pw, u + 1)
                    dve.wait_ge(s_add, (u + 1) * CHUNKS)
                    dve.wait_ge(s_lc, u + 1)
                    dve.tensor_copy(G[q][:, :, D:TW],
                                    pw_ps[:, 0:GH].rearrange("p (h t) -> p t h", h=HEADS)).then_inc(s_pc, 1)
                    dve.tensor_tensor(dr[:], carry[0:1, 0, 0:EX:TILES + 2], sm_ps[0:1, 0:GH:TILES],
                                      ALU.subtract).then_inc(s_r, 1)
                if c == 5 and part == 1:
                    dve.wait_ge(s_r, 5 * u + 2)
                    dve.tensor_scalar(dr2[:], dr[:], cont[0:1, 0:1], None, ALU.mult).then_inc(s_r, 1)
                    dve.tensor_copy(ext[0:1, 0, :, 0], carry[0:1, 0, TILES:EX:TILES + 2]).then_inc(s_r, 1)
                if c == 5 and part == 4:
                    dve.wait_ge(s_rx, u + 1)
                    dve.tensor_scalar(r1[:], rr[:], -1.0, None, ALU.add).then_inc(s_r, 1)

            carry_back = carry[:].rearrange("o k x -> o (k x)")[:, EX + 2:2 * EX + 2]
            carry_view = carry[:, :, 0:EX].rearrange("o k (h p) -> o k h p", h=HEADS)[:, :, :, 0:TILES]

            def rescale(u, off0):
                dve.wait_ge(s_rf, u + 1)
                dve.tensor_scalar(fac[:], sm_ps[:, 404:404 + HEADS], 1.0, None, ALU.add).then_inc(s_usc, 1)
                dve.wait_ge(s_usc, 3 * u + 1)
                if not isinstance(u, int) or u >= 1:
                    dve.wait_ge(s_acc, TILES * u)
                num = U[:, bass.ds(off0, D)].rearrange("p (h d) -> p h d", h=HEADS)
                dve.tensor_tensor(num, num, fac[:].unsqueeze(2).to_broadcast([P, HEADS, HD]), ALU.mult).then_inc(s_usc, 1)
                dn = U[:, bass.ds(off0 + D, HEADS)]
                dve.tensor_tensor(dn, dn, fac[:], ALU.mult).then_inc(s_usc, 1)

            def weight(q, c):
                ts = chunk_tiles(c)
                rows = G[q][:, ts[0]:ts[-1] + 1, 0:D].rearrange("p t (h d) -> p t h d", h=HEADS)
                w = pw_ps[:, 0:GH].rearrange("p (h t) -> p t h", h=HEADS)[:, ts[0]:ts[-1] + 1, :]
                dve.tensor_tensor(rows, rows, w.unsqueeze(3).to_broadcast([P, len(ts), HEADS, HD]),
                                  ALU.mult).then_inc(s_f, 1)

            def offsets(q, turn):
                dve.wait_ge(s_off[q], (turn + 1) * 16)
                settle(dve)
                return nc.values_load_multi_w_load_instructions(
                    boff[q][0:1, 0:TILES], engines=[dve.engine], min_val=0,
                    max_val=(BLK - 1) * UW,
                    skip_runtime_bounds_check_because="compact ids are below the number of nodes")[1]

            def accumulate(v, t, offs):
                dve.wait_ge(s_agg, v * TILES + t + 1)
                if t == 0:
                    dve.wait_ge(s_usc, 3 * v + 3)
                if not isinstance(v, int) or v * TILES + t >= 1:
                    dve.wait_ge(s_acc, v * TILES + t)
                two = U[:, bass.ds(offs[t], 2 * UW)]
                dve.tensor_tensor(two, two, agg_ps[t % 3][:, 0:2 * UW], ALU.add).then_inc(s_acc, 1)

            def period(s, q, turn, offs, new=True, att=True, old=True, cur=True):
                if old and offs is None:
                    offs = offsets(q, turn - 1)
                for c in range(CHUNKS):
                    v, tiles = None, []
                    if c < LAG and old:
                        v, tiles = s - 2, chunk_tiles(c + CHUNKS - LAG)
                    if c == LAG and cur:
                        if isinstance(s, int) and s == 1:
                            dve.wait_ge(s_z, 16)
                        offs = offsets(1 - q, turn - 1 + q)
                        rescale(s - 1, offs[0])
                    if c >= LAG and cur:
                        v, tiles = s - 1, chunk_tiles(c - LAG)
                    if len(tiles) > 0:
                        accumulate(v, tiles[0], offs)
                    if att:
                        attention(s - 1, 1 - q, c, 0)
                    if c + 1 < LAG and old:
                        weight(q, c + 1 + CHUNKS - LAG)
                    if c + 1 >= LAG and cur:
                        weight(1 - q, c + 1 - LAG)
                    if att:
                        attention(s - 1, 1 - q, c, 1)
                    if len(tiles) > 1:
                        accumulate(v, tiles[1], offs)
                    if att:
                        attention(s - 1, 1 - q, c, 2)
                    if new:
                        add_chunk(s, q, turn, c)
                    if att:
                        attention(s - 1, 1 - q, c, 3)
                    if len(tiles) > 2:
                        accumulate(v, tiles[2], offs)
                    if att:
                        attention(s - 1, 1 - q, c, 4)
                    if new and c == 5:
                        node_ids(s, q)
                    if new and c == 6:
                        cuts(s, q, turn)
                return offs

            period(0, 0, 0, None, att=False, old=False, cur=False)
            period(1, 1, 0, None, old=False)
            with nc.Fori(0, TURNS, engines=(dve.engine,), hint_back_edge=True) as k:
                for j in range(UNROLL):
                    offs = period(k * UNROLL + 2 + j, j % 2, k * (UNROLL // 2) + 1 + j // 2, offs if j else None)
            for i, s in enumerate(LEFT):
                offs = period(s, s % 2, s // 2, offs if i else None)
            offs = period(NS, NS % 2, NS // 2, offs, new=False)
            period(NS + 1, (NS + 1) % 2, (NS + 1) // 2, offs, new=False, att=False, cur=False)

            dve.wait_ge(s_acc, NT)
            dve.wait_ge(s_agg, NT)
            if NC > FULL:
                dve.memset(work[:, FULL * D:NC * D], 0.0).then_inc(s_w0, 1)
            ub = U[:, 0:BLK * UW].rearrange("p (b w) -> p b w", w=UW)
            den3 = den[:].rearrange("p (b h) -> p b h", h=HEADS)
            rden3 = rden[:].rearrange("p (b h) -> p b h", h=HEADS)
            dve.tensor_scalar(den3, ub[:, :, D:TW], 1.0 / BIG, None, ALU.max).then_inc(s_n, 1)
            dve.tensor_scalar(empty[:], ub[:, :, D], 0.0, float(4 * N), ALU.is_equal, ALU.mult).then_inc(s_n, 1)
            dve.wait_ge(s_n, 2)
            dve.reciprocal(rden[:], den[:]).then_inc(s_n, 1)
            dve.tensor_tensor(rowf[:], empty[:], ub[:, :, UW - 1], ALU.add).then_inc(s_n, 1)
            dve.wait_ge(s_n, 4)
            dve.tensor_copy(rowi[:], rowf[:]).then_inc(s_n, 1)
            dve.wait_ge(s_n, 5)
            for b in range(BLK):
                num = ub[:, b, 0:D].rearrange("p (h d) -> p h d", h=HEADS)
                dve.tensor_tensor(num, num, rden3[:, b, :].unsqueeze(2).to_broadcast([P, HEADS, HD]),
                                  ALU.mult).then_inc(s_nb, 1)
            for sl in range(NG + 3):
                j = sl - 3
                if j >= 0:
                    c0, k = group(j)
                    r, a = cols_in(res[j % 3], 0, k), cols_in(act_o[j % 4], 0, k)
                if sl < NG:
                    dve.wait_ge(s_re, sl + 1)
                    bn_stats(sl, act_o[sl % 4], s_dst)
                if j >= 0:
                    if j == 0:
                        dve.wait_ge(s_wd, 16 * 4)
                    dve.wait_ge(s_norm, j + 1)
                    if j >= 3:
                        dve.wait_ge(s_out[j % 3], 16 * (j // 3))
                    dve.tensor_tensor(r, a, gam[:].unsqueeze(1).to_broadcast([P, k, D]), ALU.mult).then_inc(s_res, 1)
                if 1 <= sl <= NG:
                    inverse(sl - 1, s_dsq, s_dnm)
                if j >= 0:
                    dve.wait_ge(s_res, 3 * j + 1)
                    dve.tensor_tensor(r, r, bet[:].unsqueeze(1).to_broadcast([P, k, D]), ALU.add).then_inc(s_res, 1)
                if sl < NG:
                    bn_aggr(sl, s_dst)
                if 1 <= sl <= NG:
                    minus_mean(sl - 1, s_dnm)
                if j >= 0:
                    dve.wait_ge(s_res, 3 * j + 2)
                    if j == 0:
                        dve.wait_ge(s_xd, 16 * (1 + (NC > FULL)))
                    dve.tensor_tensor(r, r, cols_in(work, c0, c0 + k), ALU.add).then_inc(s_res, 1)

        @block.scalar
        def _(act):
            act.wait_ge(s_blk, 1)
            for i in range(HEADS):
                act.dma_start(ablk[i * HD:(i + 1) * HD, i:i + 1],
                              attn[i:i + 1, :].rearrange("a d -> d a")).then_inc(s_w, 16)
            act.dma_start(bcol[:], b_proj.rearrange("a d -> d a")).then_inc(s_w, 16)
            act.dma_start(wnat[:], w_nat).then_inc(s_w, 16)
            act.dma_start(wx[:, 0:D], w_t[0:D, :]).then_inc(s_w, 16)
            act.dma_start(we[:, 0:D], w_t[D:D + ED, :]).then_inc(s_w, 16)
            act.dma_start(bias[:, 0:D], b_proj.to_broadcast([P, D])).then_inc(s_w, 16)
            act.dma_start(wo[:], wo_t).then_inc(s_wd, 16)
            act.dma_start(bo[:], b_out).then_inc(s_wd, 16)
            act.dma_start(gam[:], gamma.to_broadcast([P, D])).then_inc(s_wd, 16)
            act.dma_start(bet[:], beta.to_broadcast([P, D])).then_inc(s_wd, 16)
            act.wait_ge(s_h0, 1)

            def deviations(g, moments, done):
                c0, k = group(g)
                act.wait_ge(moments, 2 * g + 2)
                act.activation(sd[:, c0:c0 + k], mv[:, c0:c0 + k, 1], ACT.Sqrt, bias=eps[:, 0:1]).then_inc(done, 1)

            def columns(g, ready, done):
                act.wait_ge(ready, g + 1)
                n = group(g)[1] * P
                act.copy(colT[g % 2][:, 0:n], ps[g % 2][:, 0:n]).then_inc(done, 1)

            for sl in range(SLOTS):
                if sl < NG:
                    deviations(sl, s_st, s_sq)
                if 3 <= sl < NG + 3:
                    if sl >= 5:
                        act.wait_ge(s_hp, sl - 4)
                    columns(sl - 3, s_hT, s_hTc)
                if 1 <= sl <= NG:
                    c0, k = group(sl - 1)
                    act.wait_ge(s_nm, 2 * (sl - 1) + 2)
                    for i in range(c0, c0 + k):
                        col = h[:, i * D:(i + 1) * D]
                        ins = act.activation(col, col, ACT.Relu, bias=nmr[:, i:i + 1], scale=rstd[:, i:i + 1])
                    ins.then_inc(s_ac, 1)
                b = sl - IDS_SLOT - 1
                if 0 <= b < NBT:
                    act.wait_ge(s_segt, b + 2)
                    t0, t1 = b * BT, min(b * BT + BT, TILES)
                    act.copy(ncrel_all[:, t0:t1, :],
                             ps[6 + b % 2][:, 0:(t1 - t0) * NS].rearrange("p (t s) -> p t s", s=NS)).then_inc(s_segc, 1)
            act.wait_ge(s_segc, NBT)

            def ids_of(s, q):
                if not isinstance(s, int) or s >= 2:
                    act.wait_ge(s_sel, (s - 1) * CHUNKS)
                    act.wait_ge(s_r, (s - 1) * 5)
                act.copy(ncrel[q][:], ncrel_all[:, :, bass.ds(s, 1)].rearrange("p t o -> p (t o)")).then_inc(s_ncr, 1)

            def select(v, q, cc):
                peel = isinstance(v, int)
                ts = chunk_tiles(cc)
                if cc == 0:
                    act.wait_ge(s_ncr, v + 1)
                if not peel or v * CHUNKS + cc >= 2:
                    act.wait_ge(s_sel, v * CHUNKS + cc - 1)
                par = (q * CHUNKS + cc) % 2
                for i, t in enumerate(ts):
                    act.activation(dist[par][:, i, :], iota[:], ACT.Abs, bias=ncrel[q][:, t:t + 1]).then_inc(s_dist, 1)
                act.wait_ge(s_dist, v * TILES + ts[-1] + 1)
                if not peel or v * CHUNKS + cc >= 3:
                    back = chunk_tiles((cc - 3) % CHUNKS)[-1] + 1 - (TILES if cc < 3 else 0)
                    act.wait_ge(s_agg, v * TILES + back)
                act.activation(sel[cc % 3][:, 0:len(ts), :], dist[par][:, 0:len(ts), :], ACT.Relu,
                               bias=1.0, scale=-1.0).then_inc(s_sel, 1)

            def attention(u, q, c):
                if c == 0:
                    act.wait_ge(s_add, (u + 1) * CHUNKS)
                    if not isinstance(u, int) or u >= 1:
                        act.wait_ge(s_lt, u)
                    act.copy(lc[:].rearrange("p (h t) -> p h t", h=HEADS),
                             G[q][:, :, D:TW].rearrange("p t h -> p h t")).then_inc(s_lc, 1)
                if c == 4:
                    act.wait_ge(s_mx, 5 * u + 5)
                    if not isinstance(u, int) or u >= 1:
                        act.wait_ge(s_pw, u)
                    act.activation(pt[:], dd[:], ACT.Exp).then_inc(s_exp, 1)
                if c == 5:
                    act.wait_ge(s_r, 5 * u + 3)
                    act.activation(rr[:], dr2[:], ACT.Exp).then_inc(s_rx, 1)

            def period(s, q, new=True, att=True, old=True, cur=True):
                for c in range(CHUNKS):
                    if c + 2 < LAG and old:
                        select(s - 2, q, c + 2 + CHUNKS - LAG)
                    if c + 2 >= LAG and cur:
                        select(s - 1, 1 - q, c + 2 - LAG)
                    if att:
                        attention(s - 1, 1 - q, c)
                    if new and c == LAG:
                        ids_of(s, q)

            period(0, 0, att=False, old=False, cur=False)
            period(1, 1, old=False)
            with nc.Fori(0, TURNS, engines=(act.engine,), hint_back_edge=True) as k:
                for j in range(UNROLL):
                    period(k * UNROLL + 2 + j, j % 2)
            for s in LEFT:
                period(s, s % 2)
            period(NS, NS % 2, new=False)
            period(NS + 1, (NS + 1) % 2, new=False, att=False, cur=False)
            for sl in range(NG + 3):
                if sl < NG:
                    if sl >= 2:
                        act.wait_ge(s_o, sl - 1)
                    columns(sl, s_yT, s_yTc)
                if 1 <= sl <= NG:
                    j = sl - 1
                    act.wait_ge(s_o, j + 1)
                    if j >= 4:
                        act.wait_ge(s_res, 3 * (j - 4) + 1)
                    act.activation(act_o[j % 4][:, 0:group(j)[1] * D], ps[2 + j % 2][:, 0:group(j)[1] * D],
                                   ACT.Relu).then_inc(s_re, 1)
                if 2 <= sl < NG + 2:
                    deviations(sl - 2, s_dst, s_dsq)
                if sl >= 3:
                    j = sl - 3
                    c0, k = group(j)
                    act.wait_ge(s_dnm, 2 * j + 2)
                    for i in range(k):
                        col = act_o[j % 4][:, i * D:(i + 1) * D]
                        ins = act.activation(col, col, ACT.Identity, bias=nmr[:, c0 + i:c0 + i + 1],
                                             scale=rstd[:, c0 + i:c0 + i + 1])
                    ins.then_inc(s_norm, 1)


def arrange(x, src, dst, edge_attr_64, W_proj_w, W_proj_b, attn_vec, W_out_w, W_out_b, ln_gamma, ln_beta):
    import numpy as np

    E = src.shape[0]
    ns = E // SE
    padded = np.pad(dst, 1, constant_values=-1)
    t = lambda a: a.reshape(ns, TILES, P).transpose(0, 2, 1)
    meta = np.concatenate([t(src), t(dst), t(padded[:E])], axis=2)
    after = lambda n, k: padded[k::n][:E // n, None]
    win = np.concatenate([padded[:E].reshape(-1, P), after(P, P), after(P, P + 1)], axis=1).reshape(ns, 1, TILES, P + 2)
    seg = np.broadcast_to(win, (ns, HEADS, TILES, P + 2)).reshape(ns, GH, P + 2)
    dq = np.concatenate([padded[:E].reshape(ns, SE), after(SE, SE)], axis=1)
    ef = edge_attr_64.reshape(ns, SE, ED).transpose(0, 2, 1)
    row = lambda a: a.reshape(1, -1)
    named = dict(x=x, meta=meta, seg=seg, dq=dq, ef=ef, w_nat=W_proj_w, w_t=W_proj_w.T, b_proj=row(W_proj_b),
                 attn=attn_vec, wo_t=W_out_w.T, b_out=row(W_out_b), gamma=row(ln_gamma), beta=row(ln_beta))
    return {f"in_{k}": np.ascontiguousarray(v) for k, v in named.items()}


def kernel(**inputs):
    import numpy as np
    import concourse.bacc as bacc
    from concourse.bass_utils import run_bass_kernel_spmd

    ins = {k.replace("L0_gnn_", ""): np.asarray(v) for k, v in inputs.items()}
    arrays = arrange(**ins)
    nc = bacc.Bacc("TRN2", target_bir_lowering=False, num_devices=1)
    args = [nc.dram_tensor(k, a.shape, mybir.dt.from_np(a.dtype), kind="ExternalInput").ap() for k, a in arrays.items()]
    out = nc.dram_tensor("out_h", ins["x"].shape, F32, kind="ExternalOutput").ap()
    gnn_layer(nc, *args, out)
    return run_bass_kernel_spmd(nc, [arrays], core_ids=[0]).results[0]["out_h"]
```
